# Optimizing a Trainium2 kernel written in Bass

```python
import numpy as np
import jax
import jax.numpy as jnp

def _softmax(x, axis=-1):
    return jax.nn.softmax(x, axis=axis)

def _gelu(x):
    return jax.nn.gelu(x, approximate=True)

def _silu(x):
    return jax.nn.silu(x)

def _sigmoid(x):
    return jax.nn.sigmoid(x)

def _layernorm(x, axis=-1, eps=1e-05):
    m = jnp.mean(x, axis=axis, keepdims=True)
    v = jnp.var(x, axis=axis, keepdims=True)
    return (x - m) / jnp.sqrt(v + eps)

def _scatter_add(tgt, idx, src, axis=0):
    return tgt.at[idx].add(src)

def _segment_sum(src, seg, n):
    return jax.ops.segment_sum(src, seg, n)
kernel_name = 'mk_sandwich_d1_jaxref_r4_87326c'

def setup_inputs(seed: int=0):
    np.random.seed(seed)
    _w = jnp.asarray

    def _L0_attn_setup():
        import jax, jax.numpy as jnp
        import numpy as np
        ROPE_THETA = 10000.0
        INF_APPROX = 1e+30
        D_HEAD = 128

        def _rope(x, theta=ROPE_THETA):
            *_, L, D = x.shape
            half = D // 2
            pos = jnp.arange(L, dtype=jnp.float32)[:, None]
            freqs = jnp.power(theta, -jnp.arange(half, dtype=jnp.float32) / half)[None, :]
            angles = pos * freqs
            cos = jnp.cos(angles).astype(x.dtype)
            sin = jnp.sin(angles).astype(x.dtype)
            even, odd = jnp.split(x, 2, axis=-1)
            r_even = even * cos - odd * sin
            r_odd = even * sin + odd * cos
            return jnp.concatenate([r_even, r_odd], axis=-1)
        key = jax.random.key(seed)
        kx, kq, kk, kv, ko = jax.random.split(key, 5)
        B, T, M, D, G, H = (2, 256, 512, 128, 4, 4)
        std_m = M ** (-0.5)
        std_d = D ** (-0.5)
        return {'x': jax.random.normal(kx, (B, T, M), jnp.float32), 'w_aq': jax.random.normal(kq, (G, H, M, D), jnp.float32) * std_m, 'w_ak': jax.random.normal(kk, (G, M, D), jnp.float32) * std_m, 'w_av': jax.random.normal(kv, (G, M, D), jnp.float32) * std_m, 'w_ao': jax.random.normal(ko, (G, H, D, M), jnp.float32) * std_d}
    _L0_attn_in = _L0_attn_setup()

    def _L0_ffn_setup():
        import jax, jax.numpy as jnp
        import numpy as np
        from jax import lax
        H = 512
        I = 256
        E = 32
        K = 4
        SH_I = 512
        EPS = 1e-06

        def _rmsnorm(x, w, eps=EPS):
            var = jnp.mean(jnp.square(x.astype(jnp.float32)), axis=-1, keepdims=True)
            return (x * lax.rsqrt(var + eps)).astype(x.dtype) * w
        key = jax.random.key(seed)
        ks = jax.random.split(key, 8)
        s = lambda d: 1.0 / np.sqrt(d)
        return {'x': jax.random.normal(ks[0], (2, 512, H), jnp.float32), 'norm_w': jnp.ones((H,), jnp.float32), 'router_w': jax.random.normal(ks[1], (E, H), jnp.float32) * s(H), 'w1': jax.random.normal(ks[2], (E, H, 2 * I), jnp.float32) * s(H), 'w2': jax.random.normal(ks[3], (E, I, H), jnp.float32) * s(I), 'sg': jax.random.normal(ks[4], (H, SH_I), jnp.float32) * s(H), 'su': jax.random.normal(ks[5], (H, SH_I), jnp.float32) * s(H), 'sd': jax.random.normal(ks[6], (SH_I, H), jnp.float32) * s(SH_I)}
    _L0_ffn_in = _L0_ffn_setup()
    _d = {'L0_attn_x': _L0_attn_in['x'], 'L0_attn_w_aq': _L0_attn_in['w_aq'], 'L0_attn_w_ak': _L0_attn_in['w_ak'], 'L0_attn_w_av': _L0_attn_in['w_av'], 'L0_attn_w_ao': _L0_attn_in['w_ao'], 'L0_ffn_norm_w': _L0_ffn_in['norm_w'], 'L0_ffn_router_w': _L0_ffn_in['router_w'], 'L0_ffn_w1': _L0_ffn_in['w1'], 'L0_ffn_w2': _L0_ffn_in['w2'], 'L0_ffn_sg': _L0_ffn_in['sg'], 'L0_ffn_su': _L0_ffn_in['su'], 'L0_ffn_sd': _L0_ffn_in['sd']}
    _x0 = _d['L0_attn_x']
    _d['L0_attn_x'] = jax.random.normal(jax.random.fold_in(jax.random.key(seed), 1), (4, 1024, 512), dtype=_x0.dtype)
    del _x0
    return _d

def reference(L0_attn_x, L0_attn_w_aq, L0_attn_w_ak, L0_attn_w_av, L0_attn_w_ao, L0_ffn_norm_w, L0_ffn_router_w, L0_ffn_w1, L0_ffn_w2, L0_ffn_sg, L0_ffn_su, L0_ffn_sd):

    def _L0_attn_ref(x, w_aq, w_ak, w_av, w_ao):
        import jax, jax.numpy as jnp
        import numpy as np
        ROPE_THETA = 10000.0
        INF_APPROX = 1e+30
        D_HEAD = 128

        def _rope(x, theta=ROPE_THETA):
            *_, L, D = x.shape
            half = D // 2
            pos = jnp.arange(L, dtype=jnp.float32)[:, None]
            freqs = jnp.power(theta, -jnp.arange(half, dtype=jnp.float32) / half)[None, :]
            angles = pos * freqs
            cos = jnp.cos(angles).astype(x.dtype)
            sin = jnp.sin(angles).astype(x.dtype)
            even, odd = jnp.split(x, 2, axis=-1)
            r_even = even * cos - odd * sin
            r_odd = even * sin + odd * cos
            return jnp.concatenate([r_even, r_odd], axis=-1)
        B, T, M = x.shape
        q = jnp.einsum('bim,ghmd->bghid', x, w_aq)
        k = jnp.einsum('bim,gmd->bgid', x, w_ak)
        v = jnp.einsum('bim,gmd->bgid', x, w_av)
        q = _rope(q)
        k = _rope(k)
        qk_mult = jnp.asarray(D_HEAD ** (-0.25), dtype=x.dtype)
        s = jnp.einsum('bghid,bgjd->bghij', q * qk_mult, k * qk_mult)
        i = jnp.arange(T)[:, None]
        j = jnp.arange(T)[None, :]
        mask = (i < j).astype(s.dtype)
        s = s - jnp.asarray(INF_APPROX, dtype=s.dtype) * mask
        p = jax.nn.softmax(s, axis=-1)
        o = jnp.einsum('bghij,bgjd->bghid', p, v)
        r = jnp.einsum('bghid,ghdm->bim', o, w_ao)
        return r

    def _L0_ffn_ref(x, norm_w, router_w, w1, w2, sg, su, sd):
        import jax, jax.numpy as jnp
        import numpy as np
        from jax import lax
        H = 512
        I = 256
        E = 32
        K = 4
        SH_I = 512
        EPS = 1e-06

        def _rmsnorm(x, w, eps=EPS):
            var = jnp.mean(jnp.square(x.astype(jnp.float32)), axis=-1, keepdims=True)
            return (x * lax.rsqrt(var + eps)).astype(x.dtype) * w
        B, S, _ = x.shape
        residual = x
        h = _rmsnorm(x, norm_w)
        flat = h.reshape(-1, H)
        T = flat.shape[0]
        logits = flat.astype(jnp.float32) @ router_w.T
        scores = jax.nn.softmax(logits, axis=-1)
        topk_w, topk_ids = lax.top_k(scores, K)
        topk_w = topk_w / jnp.sum(topk_w, axis=-1, keepdims=True)
        ids = topk_ids.reshape(-1)
        sort_idx = jnp.argsort(ids)
        tok_idx = sort_idx // K
        xs = jnp.take(flat, tok_idx, axis=0)
        group_sizes = jnp.bincount(ids, length=E).astype(jnp.int32)
        gu = lax.ragged_dot(xs, w1, group_sizes)
        g, u = jnp.split(gu, 2, axis=-1)
        act = jax.nn.silu(g) * u
        ys = lax.ragged_dot(act, w2, group_sizes)
        y = jnp.zeros((T * K, H), ys.dtype).at[sort_idx].set(ys)
        routed = jnp.sum(y.reshape(T, K, H) * topk_w[..., None].astype(ys.dtype), axis=1)
        shared = jax.nn.silu(flat @ sg) * (flat @ su) @ sd
        out = residual + (routed + shared).reshape(B, S, H)
        return out
    x = L0_attn_x
    x = x + _layernorm(_L0_attn_ref(_layernorm(x, axis=-1), L0_attn_w_aq, L0_attn_w_ak, L0_attn_w_av, L0_attn_w_ao), axis=-1)
    x = x + _layernorm(_L0_ffn_ref(_layernorm(x, axis=-1), L0_ffn_norm_w, L0_ffn_router_w, L0_ffn_w1, L0_ffn_w2, L0_ffn_sg, L0_ffn_su, L0_ffn_sd), axis=-1)
    return x

_drawn_inputs = setup_inputs


def setup_inputs(seed=0):
    import zlib

    import numpy as np

    out = dict(_drawn_inputs(seed))
    spreads = {'L0_ffn_norm_w': (1.0, 0.2)}
    factors = {}
    for name, (base, spread) in spreads.items():
        noise = np.random.default_rng([zlib.crc32(name.encode()), seed]).standard_normal(out[name].shape)
        drawn = base * np.exp(spread * noise) if base else spread * noise
        out[name] = jnp.asarray(drawn.astype(out[name].dtype))
    for name, factor in factors.items():
        out[name] = (out[name] * factor).astype(out[name].dtype)
    return out
```

```python
from contextlib import ExitStack

import concourse.bass as bass
from concourse import mybir

ALU = mybir.AluOpType
ACT = mybir.ActivationFunctionType
AX_X = mybir.AxisListType.X
F32 = mybir.dt.float32
F32R = mybir.dt.float32r
BF16 = mybir.dt.bfloat16
I32 = mybir.dt.int32
U32 = mybir.dt.uint32

P = 128
B, T, M = 4, 1024, 512
G, H, D = 4, 4, 128
MC = M // P
NT = T // P
NTOK = B * T
NTILE = NTOK // P
E, K = 32, 4
FI = 256
FS = 512
QW = H * D
PW = QW + 2 * D
RW = QW + D
HALF = D // 2
LN_EPS, RMS_EPS = 1e-5, 1e-6
MASKED = -1e30
XT = NTOK * K // P + E
XW = XT + 2

IB = 2
NIB = NT // IB
UNITS = [(ib, h) for ib in range(NIB) for h in range(H)]
PAIRS = [(u, jp) for u, (ib, h) in enumerate(UNITS) for jp in range(ib + 1)]
NPAIR = len(PAIRS)
PAIR_OF = {p: n for n, p in enumerate(PAIRS)}

SG = NT + 2 * len(UNITS)
TG = 2 * NT + NPAIR
MG = len(UNITS) + NT
TB = NT + G * TG + NT
MB = G * MG + NT

C_ID, C_MASK, C_TRI, C_COS, C_SIN, C_NSIN, C_IOTA, C_TOK = 0, 128, 256, 384, 896, 1408, 1920, 2112
C_W = 2144


def wait_apart(eng, sem, value):
    value = eng.to_reg(value)
    eng.wait_ge(sem, 1)
    eng.wait_ge(sem, value)


def flatten(t):
    return t[:].rearrange("p c n -> p (c n)")


def misc_index(u=None, rt=None):
    order = []
    for n, (ib, h) in enumerate(UNITS):
        if h == 0 and ib > 0:
            order += [("r", IB * (ib - 1) + a) for a in range(IB)]
        order.append(("o", n))
    order += [("r", IB * (NIB - 1) + a) for a in range(IB)]
    return order.index(("o", u) if rt is None else ("r", rt))


def attention(nc, x, w_aq, w_ak, w_av, w_ao, norm_w, router_w, const, x2_d, h0_d, h_d, top, topi):
    with ExitStack() as ctx:
        def sb(name, shape, dt=F32):
            return ctx.enter_context(nc.sbuf_tensor(name, shape, dt))

        def sem(name):
            return ctx.enter_context(nc.semaphore(name))

        cst = sb("cst", [P, C_IOTA])
        xTh, xTl = sb("xTh", [P, MC, T], F32R), sb("xTl", [P, MC, T], F32R)
        qTh, qTl = sb("qTh", [P, H, T], F32R), sb("qTl", [P, H, T], F32R)
        kTh, kTl = sb("kTh", [P, T], F32R), sb("kTl", [P, T], F32R)
        vh, vl = sb("vh", [P, NT, D], F32R), sb("vl", [P, NT, D], F32R)
        wph, wpl = sb("wph", [P, MC, PW], F32R), sb("wpl", [P, MC, PW], F32R)
        woh, wol = sb("woh", [P, H, M], F32R), sb("wol", [P, H, M], F32R)
        stage = sb("stage", [P, 2, M])
        prob = sb("prob", [P, 2, IB, T])
        pth, ptl = sb("pth", [P, 2, M], F32R), sb("ptl", [P, 2, M], F32R)
        oTh, oTl = sb("oTh", [P, H, IB * P], F32R), sb("oTl", [P, H, IB * P], F32R)
        racc = sb("racc", [P, NT, M])
        work = sb("work", [P, NT, M])
        hT = sb("hT", [P, 2, M])
        lgt = sb("lgt", [P, NT, E])
        rwT = sb("rwT", [P, MC, E])
        nwb = sb("nwb", [P, M])
        idb, mskb = sb("idb", [P, P], BF16), sb("mskb", [P, P], BF16)
        stat = sb("stat", [P, NT, 6])
        mv = sb("mv", [P, NT, 2])
        vareps, std, rstd = sb("vareps", [P, NT]), sb("std", [P, NT]), sb("rstd", [P, NT])
        ssq = sb("ssq", [P, NT])
        negmax, rsum, rinv = sb("negmax", [P, 4]), sb("rsum", [P, 4]), sb("rinv", [P, 4])
        top8, idx8 = sb("top8", [P, NT, 8]), sb("idx8", [P, NT, 8], U32)

        S = ctx.enter_context(nc.psum_tensor("S", [P, 2, 1024], F32))
        TP = ctx.enter_context(nc.psum_tensor("TP", [P, 2, 512], F32))
        O = ctx.enter_context(nc.psum_tensor("O", [P, 2, 512], F32))

        rw = hT[0:E, 0]
        flat = work[:].rearrange("p t m -> p (t m)")
        raw = [flat[:, i * PW:(i + 1) * PW] for i in range(2)]
        t1 = [flat[:, 2 * PW + i * RW:2 * PW + (i + 1) * RW] for i in range(2)]
        t2 = [flat[:, 2 * PW + (2 + i) * RW:2 * PW + (3 + i) * RW] for i in range(2)]
        xin = prob[:].rearrange("p a b t -> p (a b t)").rearrange("p (t m) -> p t m", m=M)
        ident = cst[:, C_ID:C_ID + P]
        cos = cst[:, C_COS:C_COS + NT * HALF].rearrange("p (t c) -> p t c", t=NT)
        sin = cst[:, C_SIN:C_SIN + NT * HALF].rearrange("p (t c) -> p t c", t=NT)
        nsin = cst[:, C_NSIN:C_NSIN + NT * HALF].rearrange("p (t c) -> p t c", t=NT)

        const_in = sem("const_in")
        x_in = sem("x_in")
        stored = sem("stored")
        staged = [sem("staged0"), sem("staged1")]
        stage_free = sem("stage_free")
        w_hi = sem("w_hi")
        cast_ready = sem("cast_ready")
        rwT_ps, rwT_sb = sem("rwT_ps"), sem("rwT_sb")
        var_ready, std_ready = sem("var_ready"), sem("std_ready")
        dve = sem("dve")
        xln_ready = sem("xln_ready")
        s_done = sem("s_done")
        s_read = sem("s_read")
        turned = sem("turned")
        crossed = sem("crossed")
        tp_done, tp_hi, tp_lo = sem("tp_done"), sem("tp_hi"), sem("tp_lo")
        max_ready, rinv_ready, p_ready = sem("max_ready"), sem("rinv_ready"), sem("p_ready")
        pv_done = sem("pv_done")
        o_hi = sem("o_hi")
        o_free = sem("o_free")
        r_done = sem("r_done")
        lg_done = sem("lg_done")
        h_ready = sem("h_ready")
        out_ready = sem("out_ready")
        placed = sem("placed")
        sq_ready, sq_done = sem("sq_ready"), sem("sq_done")

        block = ctx.enter_context(nc.Block())

        @block.sync
        def _(sp):
            sp.dma_start(cst[:], const[:, 0:C_IOTA]).then_inc(const_in, 16)
            sp.dma_start(rw, router_w).then_inc(const_in, 16)
            sp.dma_start(nwb[:], norm_w.rearrange("(a m) -> a m", a=1).to_broadcast([P, M])).then_inc(const_in, 16)

            def load_out(it, g):
                for h in range(H):
                    sp.wait_ge(stage_free, it * 10 + 6 + h + 1)
                    sp.dma_start(stage[:, h % 2], w_ao[g, h]).then_inc(staged[h % 2], 16)

            def load_proj(free, g):
                for n in range(MC + 2):
                    sp.wait_ge(stage_free, free + n + 1)
                    if n < MC:
                        dst = stage[:, n % 2].rearrange("p (h d) -> p h d", h=H)
                        src = w_aq[g, :, n * P:(n + 1) * P, :].rearrange("h p d -> p h d")
                    else:
                        dst = stage[:, n % 2].rearrange("p (c d) -> p c d", c=MC)
                        src = (w_ak if n == MC else w_av)[g].rearrange("(c p) d -> p c d", p=P)
                    sp.dma_start(dst, src).then_inc(staged[n % 2], 16)

            load_proj(0, 0)
            sp.dma_start(xin, x[0].rearrange("(t p) m -> p t m", p=P)).then_inc(x_in, 16)
            with sp.Fori(0, B) as b:
                with sp.Fori(0, G) as g:
                    it = sp.snap(b * G + g)
                    load_out(it, g)
                    load_proj(it * 10 + 10, (g + 1) % G)
                sp.wait_ge(tp_done, b * TB + (NT + G * TG))
                sp.dma_start(xin, x[b].rearrange("(t p) m -> p t m", p=P)).then_inc(x_in, 16)
                sp.wait_ge(out_ready, b * 2 + 2)
                sp.wait_ge(h_ready, b * NT + NT)
                sp.dma_start(x2_d[b].rearrange("(t p) m -> p t m", p=P), racc[:]).then_inc(stored, 16)
                sp.dma_start(h0_d[b].rearrange("(t p) m -> p t m", p=P), xin).then_inc(stored, 16)
                sp.dma_start(h_d[b].rearrange("(t p) m -> p t m", p=P), work[:]).then_inc(stored, 16)
                sp.wait_ge(stored, b * 48 + 48)
                sp.dma_start(xin, x[(b + 1) % B].rearrange("(t p) m -> p t m", p=P)).then_inc(x_in, 16)
            sp.wait_ge(x_in, 16 * (2 * B + 1))

        @block.gpsimd
        def _(pool):
            pool.sem_inc(stage_free, 2)

            def split(hi, lo, n, base, used):
                src = stage[:, n % 2]
                if len(hi.shape) == 3:
                    src = src.rearrange("p (c d) -> p c d", c=hi.shape[1])
                wait_apart(pool, staged[n % 2], used)
                nc.gpsimd.tensor_scalar(hi, src, 1.0, 1.0, ALU.mult, ALU.mult).then_inc(w_hi, 1)
                pool.wait_ge(w_hi, base + 1)
                nc.gpsimd.tensor_tensor(lo, src, hi.bitcast(F32), ALU.subtract).then_inc(stage_free, 1)

            def split_proj(base, dma):
                for n in range(MC + 2):
                    cols = (n, slice(0, QW)) if n < MC else (slice(0, MC), slice(QW + (n - MC) * D, QW + (n - MC + 1) * D))
                    split(wph[:, cols[0], cols[1]], wpl[:, cols[0], cols[1]], n, base + n, dma + 16 * (n // 2 + 1))

            split_proj(0, 0)
            with pool.Fori(0, B) as b:
                with pool.Fori(0, G) as g:
                    it = pool.snap(b * G + g)
                    for t in range(NT):
                        pool.wait_ge(s_read, it * SG + t + 1 + 2)
                        pool.wait_ge(const_in, 48)
                        if t >= 2:
                            pool.wait_ge(turned, it * NT + t - 1)
                        src = raw[t % 2][:, 0:RW].rearrange("p (h s c) -> p h s c", s=2, c=HALF)
                        dst = t2[t % 2].rearrange("p (h s c) -> p h s c", s=2, c=HALF)
                        tab = [nsin[:, t:t + 1, :].to_broadcast([P, H + 1, HALF]), sin[:, t:t + 1, :].to_broadcast([P, H + 1, HALF])]
                        nc.gpsimd.tensor_tensor(dst[:, :, 0, :], src[:, :, 1, :], tab[0], ALU.mult)
                        nc.gpsimd.tensor_tensor(dst[:, :, 1, :], src[:, :, 0, :], tab[1], ALU.mult).then_inc(crossed, 1)
                    pool.wait_ge(r_done, it * NT + 1)
                    for h in range(H):
                        split(woh[:, h], wol[:, h], h, it * 10 + 6 + h, it * 80 + 48 + 16 * (h // 2 + 1))
                    pool.wait_ge(s_done, it * SG + NT)
                    split_proj(it * 10 + 10, it * 80 + 80)

        @block.vector
        def _(v):
            v.sem_inc(tp_lo, 2)
            v.sem_inc(o_free, 2)
            v.wait_ge(const_in, 48)
            nc.vector.tensor_copy(idb[:], ident)
            nc.vector.tensor_copy(mskb[:], cst[:, C_MASK:C_MASK + P]).then_inc(cast_ready, 1)
            v.wait_ge(rwT_ps, 1)
            nc.vector.tensor_copy(rwT[:], TP[:, 0, 0:MC * E].rearrange("p (c e) -> p c e", c=MC)).then_inc(rwT_sb, 1)

            GD = NT * 2
            DVB = 3 * 2 * NT + 4 + 1 + NT + NT + 1 + G * GD

            def router(t, b, base, k):
                n = G * MG + t
                v.wait_ge(lg_done, b * NT + t + 1)
                nc.vector.tensor_copy(lgt[:, t], O[:, n % 2, 0:E]).then_inc(o_free, 1)
                wait_apart(v, o_free, b * MB + (n + 1 + 2))
                nc.vector.max(top8[:, t], lgt[:, t]).then_inc(dve, 1)
                wait_apart(v, dve, base + (k + 1))
                nc.vector.max_index(idx8[:, t], top8[:, t], lgt[:, t]).then_inc(placed, 1)
                return k + 1

            def link(ins, base, k):
                ins.then_inc(dve, 1)
                v.wait_ge(dve, base + (k + 1))
                return k + 1

            def stats(src_of, base, k):
                for t in range(NT):
                    nc.vector.bn_stats(stat[:, t], src_of(t)).then_inc(dve, 1)
                k += NT
                wait_apart(v, dve, base + k)
                for t in range(NT):
                    nc.vector.bn_aggr(mv[:, t], stat[:, t]).then_inc(dve, 1)
                k += NT
                v.wait_ge(dve, base + k)
                return k

            def root(src, eps, scale, base, k, roots):
                nc.vector.tensor_scalar(vareps[:], src, scale, eps, ALU.mult, ALU.add).then_inc(var_ready, 1)
                v.wait_ge(std_ready, roots)
                return link(nc.vector.reciprocal(rstd[:], std[:]), base, k)

            with v.Fori(0, B) as b:
                base = v.snap(b * DVB)
                k = 0
                tpb = v.snap(b * TB)
                hib = v.snap(b * (TB - NT))
                v.wait_ge(x_in, b * 32 + 16)
                k = stats(lambda t: xin[:, t], base, k)
                k = root(mv[:, :, 1], LN_EPS, 1.0, base, k, b * 4 + 1)
                for t in range(NT):
                    nc.vector.tensor_scalar(xin[:, t], xin[:, t], mv[:, t, 0:1], rstd[:, t:t + 1],
                                            ALU.subtract, ALU.mult).then_inc(xln_ready, 1)
                nc.vector.memset(racc[:], 0.0).then_inc(dve, 1)
                k += 1
                for t in range(NT):
                    v.wait_ge(tp_hi, hib + (t + 1))
                    c4 = xTl[:, :, t * P:(t + 1) * P]
                    nc.vector.tensor_tensor(c4, TP[:, t % 2].rearrange("p (c n) -> p c n", c=MC),
                                            xTh[:, :, t * P:(t + 1) * P].bitcast(F32), ALU.subtract).then_inc(tp_lo, 1)
                k0 = k
                with v.Fori(0, G) as g:
                    it = v.snap(b * G + g)
                    gb = v.snap(base + k0 + g * GD)
                    hi0 = v.snap(hib + NT + g * TG)

                    def lo_tile(t):
                        v.wait_ge(tp_hi, hi0 + (2 * t + 1))
                        nc.vector.tensor_tensor(qTl[:, :, t * P:(t + 1) * P], TP[:, 0].rearrange("p (h n) -> p h n", h=H),
                                                qTh[:, :, t * P:(t + 1) * P].bitcast(F32), ALU.subtract).then_inc(tp_lo, 1)
                        v.wait_ge(tp_hi, hi0 + (2 * t + 2))
                        nc.vector.tensor_tensor(kTl[:, t * P:(t + 1) * P], TP[:, 1, 0:P],
                                                kTh[:, t * P:(t + 1) * P].bitcast(F32), ALU.subtract).then_inc(tp_lo, 1)

                    for t in range(NT):
                        if t >= 2:
                            lo_tile(t - 2)
                        v.wait_ge(s_read, it * SG + t + 1 + 2)
                        tab = cos[:, t:t + 1, :].to_broadcast([P, 2 * (H + 1), HALF])
                        nc.vector.tensor_tensor(t1[t % 2].rearrange("p (h c) -> p h c", c=HALF),
                                                raw[t % 2][:, 0:RW].rearrange("p (h c) -> p h c", c=HALF),
                                                tab, ALU.mult).then_inc(dve, 1)
                        nc.vector.tensor_copy(vh[:, t], raw[t % 2][:, RW:PW]).then_inc(dve, 1)
                        v.wait_ge(dve, gb + (2 * t + 2))
                        nc.vector.tensor_tensor(vl[:, t], raw[t % 2][:, RW:PW], vh[:, t].bitcast(F32), ALU.subtract)
                        v.wait_ge(crossed, it * NT + t + 1)
                        nc.vector.tensor_tensor(t1[t % 2], t1[t % 2], t2[t % 2], ALU.add).then_inc(turned, 1)
                    lo_tile(NT - 2)
                    lo_tile(NT - 1)

                    def row_max(u, a):
                        ib = UNITS[u][0]
                        n = 2 * u + a
                        v.wait_ge(s_done, it * SG + NT + n + 1)
                        nc.vector.tensor_reduce(negmax[:, n % 4:n % 4 + 1], S[:, a, 0:(IB * ib + a + 1) * P], AX_X,
                                                ALU.max, negate=True).then_inc(max_ready, 1)

                    def recip(u, a):
                        n = 2 * u + a
                        v.wait_ge(s_read, it * SG + NT + n + 1 + 2)
                        nc.vector.reciprocal(rinv[:, n % 4:n % 4 + 1], rsum[:, n % 4:n % 4 + 1]).then_inc(rinv_ready, 1)

                    def lo_pair(u, jp):
                        n = PAIR_OF[(u, jp)]
                        w = 3 * P if jp == UNITS[u][0] else 4 * P
                        v.wait_ge(tp_hi, hi0 + (2 * NT + n + 1))
                        nc.vector.tensor_tensor(ptl[:, n % 2, 0:w], TP[:, n % 2, 0:w], pth[:, n % 2, 0:w].bitcast(F32),
                                                ALU.subtract).then_inc(tp_lo, 1)

                    def lo_out(u):
                        h = UNITS[u][1]
                        v.wait_ge(o_hi, it * len(UNITS) + u + 1)
                        nc.vector.tensor_tensor(oTl[:, h], O[:, misc_index(u) % 2, 0:IB * P], oTh[:, h].bitcast(F32),
                                                ALU.subtract).then_inc(o_free, 1)

                    def add_result(t):
                        v.wait_ge(r_done, it * NT + t + 1 + 1)
                        nc.vector.tensor_tensor(racc[:, t], racc[:, t], O[:, misc_index(rt=t) % 2, :], ALU.add).then_inc(o_free, 1)

                    for u in range(2):
                        for a in range(IB):
                            row_max(u, a)
                            if u == 0:
                                recip(u, a)
                    for u, (ib, h) in enumerate(UNITS):
                        more = u + 1 < len(UNITS)
                        if more:
                            recip(u + 1, 0)
                        lo_pair(u, 0)
                        if more:
                            recip(u + 1, 1)
                        if h == 0 and ib > 0:
                            for a in range(IB):
                                add_result(IB * (ib - 1) + a)
                        for jp in range(1, ib + 1):
                            lo_pair(u, jp)
                        if u + 2 < len(UNITS):
                            row_max(u + 2, 0)
                        lo_out(u)
                        if u + 2 < len(UNITS):
                            row_max(u + 2, 1)
                    for a in range(IB):
                        add_result(IB * (NIB - 1) + a)
                k = k0
                base2 = v.snap(base + G * GD)
                v.wait_ge(x_in, b * 32 + 32)
                v.wait_ge(o_free, b * MB + (G * MG + 2))
                k = stats(lambda t: racc[:, t], base2, k)
                k = root(mv[:, :, 1], LN_EPS, 1.0, base2, k, b * 4 + 2)
                for t in range(NT):
                    nc.vector.tensor_scalar(racc[:, t], racc[:, t], mv[:, t, 0:1], rstd[:, t:t + 1],
                                            ALU.subtract, ALU.mult).then_inc(dve, 1)
                k += NT
                v.wait_ge(dve, base2 + k)
                nc.vector.tensor_tensor(racc[:], racc[:], xin, ALU.add).then_inc(out_ready, 1)
                v.wait_ge(out_ready, b * 2 + 1)
                k = stats(lambda t: racc[:, t], base2, k)
                k = root(mv[:, :, 1], LN_EPS, 1.0, base2, k, b * 4 + 3)
                for t in range(NT):
                    ins = nc.vector.tensor_scalar(xin[:, t], racc[:, t], mv[:, t, 0:1], rstd[:, t:t + 1],
                                                  ALU.subtract, ALU.mult)
                    ins.then_inc(out_ready if t == NT - 1 else sq_ready, 1)
                v.wait_ge(sq_done, b * NT + NT)
                k = root(ssq[:], RMS_EPS, 1.0 / M, base2, k, b * 4 + 4)
                for t in range(NT):
                    nc.vector.scalar_tensor_tensor(out=work[:, t], in0=xin[:, t], scalar=rstd[:, t:t + 1], in1=nwb[:],
                                                   op0=ALU.mult, op1=ALU.mult).then_inc(h_ready, 1)
                for t in range(NT):
                    v.wait_ge(tp_done, tpb + (NT + G * TG + t + 1))
                    nc.vector.tensor_copy(hT[:, t % 2], TP[:, t % 2]).then_inc(tp_lo, 1)
                    if t >= 1:
                        k = router(t - 1, b, base2, k)
                k = router(NT - 1, b, base2, k)
                wait_apart(v, placed, b * NT + NT)
                nc.vector.tensor_copy(top[:, bass.ds(b * NT, NT), :], top8[:])
                nc.vector.tensor_copy(topi[:, bass.ds(b * NT, NT), :], idx8[:]).then_inc(dve, 1)
                k += 1
                assert k + G * GD == DVB, (k + G * GD, DVB)

        @block.scalar
        def _(act):
            act.sem_inc(s_read, 2)
            with act.Fori(0, B) as b:
                act.wait_ge(var_ready, b * 4 + 1)
                nc.scalar.activation(std[:], vareps[:], ACT.Sqrt).then_inc(std_ready, 1)
                for t in range(NT):
                    act.wait_ge(tp_done, b * TB + t + 1)
                    nc.scalar.copy(xTh[:, :, t * P:(t + 1) * P], TP[:, t % 2].rearrange("p (c n) -> p c n", c=MC)).then_inc(tp_hi, 1)
                with act.Fori(0, G) as g:
                    it = act.snap(b * G + g)
                    tp0 = act.snap(b * TB + NT + g * TG)

                    def hi_tile(t):
                        act.wait_ge(tp_done, tp0 + (2 * t + 1))
                        nc.scalar.copy(qTh[:, :, t * P:(t + 1) * P], TP[:, 0].rearrange("p (h n) -> p h n", h=H)).then_inc(tp_hi, 1)
                        act.wait_ge(tp_done, tp0 + (2 * t + 2))
                        nc.scalar.copy(kTh[:, t * P:(t + 1) * P], TP[:, 1, 0:P]).then_inc(tp_hi, 1)

                    for t in range(NT):
                        act.wait_ge(s_done, it * SG + t + 1)
                        if t >= 2:
                            act.wait_ge(turned, it * NT + t - 1)
                        nc.scalar.copy(raw[t % 2], S[:, t % 2, 0:PW]).then_inc(s_read, 1)
                        if t >= 2:
                            hi_tile(t - 2)
                    hi_tile(NT - 2)
                    hi_tile(NT - 1)

                    def exp(u, a):
                        n = 2 * u + a
                        w = (IB * UNITS[u][0] + a + 1) * P
                        act.wait_ge(max_ready, it * 2 * len(UNITS) + n + 1)
                        nc.scalar.activation(prob[:, u % 2, a, 0:w], S[:, a, 0:w], ACT.Exp, bias=negmax[:, n % 4:n % 4 + 1],
                                             accum_out=rsum[:, n % 4:n % 4 + 1]).then_inc(s_read, 1)

                    def scale(u, a):
                        n = 2 * u + a
                        w = (IB * UNITS[u][0] + a + 1) * P
                        act.wait_ge(rinv_ready, it * 2 * len(UNITS) + n + 1)
                        nc.scalar.activation(prob[:, u % 2, a, 0:w], prob[:, u % 2, a, 0:w], ACT.Copy,
                                             scale=rinv[:, n % 4:n % 4 + 1]).then_inc(p_ready, 1)

                    def hi_pair(u, jp):
                        n = PAIR_OF[(u, jp)]
                        w = 3 * P if jp == UNITS[u][0] else 4 * P
                        act.wait_ge(tp_done, tp0 + (2 * NT + n + 1))
                        act.wait_ge(pv_done, it * NPAIR + n + 1)
                        nc.scalar.copy(pth[:, n % 2, 0:w], TP[:, n % 2, 0:w]).then_inc(tp_hi, 1)

                    def hi_out(u):
                        ib, h = UNITS[u]
                        act.wait_ge(pv_done, it * NPAIR + PAIR_OF[(u, ib)] + 1 + 2)
                        if h == 0:
                            act.wait_ge(r_done, it * NT + IB * ib + 1)
                        nc.scalar.copy(oTh[:, h], O[:, misc_index(u) % 2, 0:IB * P]).then_inc(o_hi, 1)

                    for a in range(IB):
                        exp(0, a)
                    for a in range(IB):
                        scale(0, a)
                    for a in range(IB):
                        exp(1, a)
                    for u, (ib, h) in enumerate(UNITS):
                        more = u + 1 < len(UNITS)
                        for jp in range(max(ib + 1, IB)):
                            if jp <= ib:
                                hi_pair(u, jp)
                            if jp < IB and more:
                                scale(u + 1, jp)
                        if u + 2 < len(UNITS):
                            exp(u + 2, 0)
                        hi_out(u)
                        if u + 2 < len(UNITS):
                            exp(u + 2, 1)
                for r in (2, 3):
                    act.wait_ge(var_ready, b * 4 + r)
                    nc.scalar.activation(std[:], vareps[:], ACT.Sqrt).then_inc(std_ready, 1)
                for t in range(NT):
                    if t < NT - 1:
                        act.wait_ge(sq_ready, b * (NT - 1) + t + 1)
                    else:
                        act.wait_ge(out_ready, b * 2 + 2)
                    nc.scalar.activation(work[:, t], xin[:, t], ACT.Square, accum_out=ssq[:, t:t + 1]).then_inc(sq_done, 1)
                act.wait_ge(var_ready, b * 4 + 4)
                nc.scalar.activation(std[:], vareps[:], ACT.Sqrt).then_inc(std_ready, 1)

        @block.tensor
        def _(pe):
            mm = nc.tensor.matmul

            def mm3(out, ah, al, bh, bl, first, last):
                mm(out, ah, bh, start=first, stop=False)
                mm(out, ah, bl, start=False, stop=False)
                return mm(out, al, bh, start=False, stop=last)

            pe.sem_inc(pv_done, 2)
            pe.sem_inc(r_done, 1)
            pe.wait_ge(const_in, 48)
            for c in range(MC):
                ins = nc.tensor.transpose(TP[:, 0, c * E:(c + 1) * E], rw[:, c * P:(c + 1) * P], cst[0:E, C_ID:C_ID + E])
            ins.then_inc(rwT_ps, 1)
            pe.wait_ge(rwT_sb, 1)
            pe.wait_ge(cast_ready, 1)
            with pe.Fori(0, B) as b:
                tpb = pe.snap(b * TB)
                mb = pe.snap(b * MB)
                for t in range(NT):
                    pe.wait_ge(xln_ready, b * NT + t + 1)
                    pe.wait_ge(tp_lo, tpb + (t + 1))
                    for c in range(MC):
                        ins = nc.tensor.transpose(TP[:, t % 2, c * P:(c + 1) * P], xin[:, t, c * P:(c + 1) * P], ident)
                    ins.then_inc(tp_done, 1)
                with pe.Fori(0, G) as g:
                    it = pe.snap(b * G + g)
                    tp0 = pe.snap(tpb + NT + g * TG)
                    m0 = pe.snap(mb + g * MG)

                    def project(t):
                        if t == 0:
                            pe.wait_ge(tp_lo, tpb + (NT + 2))
                            pe.wait_ge(stage_free, it * 10 + 6 + 2)
                        pe.wait_ge(s_read, it * SG + t + 1)
                        tok = slice(t * P, (t + 1) * P)
                        for c in range(MC):
                            first, last = c == 0, c == MC - 1
                            for cols in (slice(0, QW), slice(QW, PW)):
                                ins = mm3(S[:, t % 2, cols], xTh[:, c, tok], xTl[:, c, tok], wph[:, c, cols], wpl[:, c, cols], first, last)
                        ins.then_inc(s_done, 1)

                    def transpose_tile(t):
                        pe.wait_ge(turned, it * NT + t + 1)
                        pe.wait_ge(tp_lo, tp0 + (2 * t + 1))
                        for h in range(H):
                            ins = nc.tensor.transpose(TP[:, 0, h * P:(h + 1) * P], t1[t % 2][:, h * D:(h + 1) * D], ident)
                        ins.then_inc(tp_done, 1)
                        pe.wait_ge(tp_lo, tp0 + (2 * t + 2))
                        nc.tensor.transpose(TP[:, 1, 0:P], t1[t % 2][:, H * D:RW], ident).then_inc(tp_done, 1)

                    for t in range(NT):
                        project(t)
                        if t >= 2:
                            transpose_tile(t - 2)
                    transpose_tile(NT - 2)
                    transpose_tile(NT - 1)

                    def scores(u, a):
                        ib, h = UNITS[u]
                        i = IB * ib + a
                        n = NT + 2 * u + a
                        w = (i + 1) * P
                        if h == 0:
                            pe.wait_ge(tp_lo, tp0 + (2 * (i + 1) + 2))
                        pe.wait_ge(s_read, it * SG + n + 1)
                        q = slice(i * P, (i + 1) * P)
                        for j0 in range(0, w, 512):
                            j1 = min(j0 + 512, w)
                            tail = j1 == w
                            ins = mm3(S[:, a, j0:j1], qTh[:, h, q], qTl[:, h, q], kTh[:, j0:j1], kTl[:, j0:j1], True, not tail)
                            if tail:
                                ins = mm(S[:, a, i * P:w], idb[:], mskb[:], start=False, stop=True)
                        ins.then_inc(s_done, 1)

                    def blocks(u, jp):
                        diag = jp == UNITS[u][0]
                        return [(jj, a) for jj in range(2) for a in range(IB) if not (diag and jj == 1 and a == 0)]

                    def transpose_pair(u, jp):
                        n = PAIR_OF[(u, jp)]
                        if jp == 0:
                            pe.wait_ge(p_ready, it * 2 * len(UNITS) + 2 * u + 2)
                        pe.wait_ge(tp_lo, tp0 + (2 * NT + n + 1))
                        for m, (jj, a) in enumerate(blocks(u, jp)):
                            j = 2 * jp + jj
                            ins = nc.tensor.transpose(TP[:, n % 2, m * P:(m + 1) * P], prob[:, u % 2, a, j * P:(j + 1) * P], ident)
                        ins.then_inc(tp_done, 1)

                    def value_pair(u, jp):
                        n = PAIR_OF[(u, jp)]
                        ib = UNITS[u][0]
                        pe.wait_ge(tp_lo, tp0 + (2 * NT + n + 1 + 2))
                        if jp == 0:
                            pe.wait_ge(o_free, m0 + (misc_index(u) + 1))
                        bank = misc_index(u) % 2
                        m = 0
                        for jj in range(2):
                            a0 = 1 if (jp == ib and jj == 1) else 0
                            w = (IB - a0) * P
                            j = 2 * jp + jj
                            cols = slice(m * P, m * P + w)
                            ins = mm3(O[:, bank, a0 * P:IB * P], vh[:, j], vl[:, j], pth[:, n % 2, cols], ptl[:, n % 2, cols],
                                      jp == 0 and jj == 0, jp == ib and jj == 1)
                            m += IB - a0
                        ins.then_inc(pv_done, 1)

                    def out_project(ib, a):
                        t = IB * ib + a
                        n = misc_index(rt=t)
                        pe.wait_ge(o_free, m0 + (n + 1))
                        if a == 0:
                            pe.wait_ge(o_free, m0 + (misc_index(H * ib + H - 1) + 1 + 2))
                            pe.wait_ge(stage_free, it * 10 + 10 + 2)
                        for h in range(H):
                            ins = mm3(O[:, n % 2, :], oTh[:, h, a * P:(a + 1) * P], oTl[:, h, a * P:(a + 1) * P], woh[:, h], wol[:, h],
                                      h == 0, h == H - 1)
                        ins.then_inc(r_done, 1)

                    for u in range(2):
                        for a in range(IB):
                            scores(u, a)
                    for u, (ib, h) in enumerate(UNITS):
                        transpose_pair(u, 0)
                        if h == 0 and ib > 0:
                            for a in range(IB):
                                out_project(ib - 1, a)
                        for jp in range(1, ib + 1):
                            transpose_pair(u, jp)
                            value_pair(u, jp - 1)
                        if u + 2 < len(UNITS):
                            scores(u + 2, 0)
                        value_pair(u, ib)
                        if u + 2 < len(UNITS):
                            scores(u + 2, 1)
                    for a in range(IB):
                        out_project(NIB - 1, a)
                def route(t):
                    n = G * MG + t
                    pe.wait_ge(o_free, mb + (n + 1))
                    pe.wait_ge(tp_lo, tpb + (NT + G * TG + t + 1 + 2))
                    for c in range(MC):
                        ins = mm(O[:, n % 2, 0:E], hT[:, t % 2, c * P:(c + 1) * P], rwT[:, c], start=c == 0, stop=c == MC - 1)
                    ins.then_inc(lg_done, 1)

                for t in range(NT):
                    n = NT + G * TG + t
                    pe.wait_ge(h_ready, b * NT + t + 1)
                    pe.wait_ge(tp_lo, tpb + (n + 1))
                    for c in range(MC):
                        ins = nc.tensor.transpose(TP[:, t % 2, c * P:(c + 1) * P], work[:, t, c * P:(c + 1) * P], ident)
                    ins.then_inc(tp_done, 1)
                    if t >= 1:
                        route(t - 1)
                route(NT - 1)


def dispatch(nc, sg, su, sd, const, h0_d, h_d, base_d, top, topi, slots, gate, ids, etab, ctab):
    with ExitStack() as ctx:
        def sb(name, shape, dt=F32):
            return ctx.enter_context(nc.sbuf_tensor(name, shape, dt))

        def sem(name):
            return ctx.enter_context(nc.semaphore(name))

        cst = sb("cst2", [P, C_W])
        stage = sb("stage2", [P, 2, M])
        wh, wl = sb("wsh", [P, 3, MC, M], F32R), sb("wsl", [P, 3, MC, M], F32R)
        hb, h0b, outb = sb("hb", [P, 2, M]), sb("h0b", [P, 2, M]), sb("outb", [P, 2, M])
        hTh, hTl = sb("hTh2", [P, MC, P], F32R), sb("hTl2", [P, MC, P], F32R)
        aTh, aTl = sb("aTh2", [P, MC, P], F32R), sb("aTl2", [P, MC, P], F32R)
        sl, ac = sb("sl2", [P, FS]), sb("ac2", [P, FS])
        trib, oneb = sb("trib", [P, P], BF16), sb("oneb", [P, P], BF16)
        hot = sb("hot", [P, K, NTILE, E])
        anyb = sb("anyb", [P, NTILE, E], BF16)
        tot, cumA, cumB, place = (sb(n, [P, NTILE, E]) for n in ("tot", "cumA", "cumB", "place"))
        idxf, slotf = sb("idxf", [P, NTILE, K]), sb("slotf", [P, NTILE, K])
        sloti, tmpi = sb("sloti", [P, NTILE, K], I32), sb("tmpi", [P, NTILE, K], I32)
        tilef, posf = sb("tilef", [P, NTILE, K]), sb("posf", [P, NTILE, K])
        nti, ntf, ca, cb = sb("nti", [P, E], I32), sb("ntf", [P, E]), sb("ca", [P, E]), sb("cb", [P, E])
        par = sb("par", [P, 2], I32)
        base = sb("basef", [P, E])
        over = sb("over", [P, XW, E])
        etf = sb("etf", [P, XW])
        selp, selt = sb("selp", [P, K, P], F32R), sb("selt", [P, K, XW], F32R)
        zero = sb("zero2", [P, XW], F32R)
        gs, gr = sb("gs", [P, NTILE]), sb("gr", [P, NTILE])

        S = ctx.enter_context(nc.psum_tensor("S2", [P, 2, 512], F32))
        TP = ctx.enter_context(nc.psum_tensor("TP2", [P, 2, 512], F32))
        O = ctx.enter_context(nc.psum_tensor("O2", [P, 512], F32))
        I = ctx.enter_context(nc.psum_tensor("I2", [P, 512], F32))
        C = ctx.enter_context(nc.psum_tensor("C2", [P, 2, 512], F32))

        const_in = sem("const_in2")
        staged, stage_free, w_hi = [sem("staged20"), sem("staged21")], sem("stage_free2"), sem("w_hi2")
        h_in, h0_in = [sem("h_in0"), sem("h_in1")], [sem("h0_in0"), sem("h0_in1")]
        base_out = [sem("base_out0"), sem("base_out1")]
        step = sem("step")
        any_ready, counted = sem("any_ready"), sem("counted")
        sel_ready, listed = sem("sel_ready"), sem("listed")
        gd_ready, ge_ready = sem("gd_ready"), sem("ge_ready")
        t_done, hh_done, hl_done = sem("t_done"), sem("hh_done"), sem("hl_done")
        gu_done, silu_done, act_ready = sem("gu_done"), sem("silu_done"), sem("act_ready")
        at_done, ah_done, al_done = sem("at_done"), sem("ah_done"), sem("al_done")
        dn_done, base_ready = sem("dn_done"), sem("base_ready")

        block = ctx.enter_context(nc.Block())

        @block.sync
        def _(sp):
            sp.dma_start(cst[:], const).then_inc(const_in, 16)
            for n in range(3 * MC):
                if n >= 2:
                    sp.wait_ge(stage_free, n - 1)
                w = (sg, su, sd)[n // MC].rearrange("(c p) f -> c p f", p=P)[n % MC]
                sp.dma_start(stage[:, n % 2], w).then_inc(staged[n % 2], 16)
            for s in range(2):
                sp.sem_inc(base_out[s], 16)
            h_t = h_d.rearrange("b (t p) m -> (b t) p m", p=P)
            h0_t = h0_d.rearrange("b (t p) m -> (b t) p m", p=P)
            base_t = base_d.rearrange("(t p) m -> t p m", p=P)
            for s in range(2):
                sp.dma_start(hb[:, s], h_t[s]).then_inc(h_in[s], 16)
                sp.dma_start(h0b[:, s], h0_t[s]).then_inc(h0_in[s], 16)
            with sp.Fori(0, NTILE // 2) as j:
                for s in range(2):
                    i = sp.snap(j * 2 + s)
                    sp.wait_ge(t_done, i + 1)
                    sp.dma_start(hb[:, s], h_t[(i + 2) % NTILE]).then_inc(h_in[s], 16)
                    sp.wait_ge(base_ready, i + 1)
                    sp.dma_start(base_t[i], outb[:, s]).then_inc(base_out[s], 16)
                    sp.dma_start(h0b[:, s], h0_t[(i + 2) % NTILE]).then_inc(h0_in[s], 16)
            for s in range(2):
                sp.wait_ge(base_out[s], 16 * (NTILE // 2 + 1))
                sp.wait_ge(h0_in[s], 16 * (NTILE // 2 + 1))
                sp.wait_ge(h_in[s], 16 * (NTILE // 2 + 1))

        @block.gpsimd
        def _(pool):
            for n in range(3 * MC):
                hi, lo = wh[:, n // MC, n % MC], wl[:, n // MC, n % MC]
                pool.wait_ge(staged[n % 2], 16 * (n // 2 + 1))
                nc.gpsimd.tensor_scalar(hi, stage[:, n % 2], 1.0, 1.0, ALU.mult, ALU.mult).then_inc(w_hi, 1)
                pool.wait_ge(w_hi, n + 1)
                nc.gpsimd.tensor_tensor(lo, stage[:, n % 2], hi.bitcast(F32), ALU.subtract).then_inc(stage_free, 1)

        @block.vector
        def _(v):
            done = [0]

            def link(ins):
                done[0] += 1
                ins.then_inc(step, 1)
                v.wait_ge(step, done[0])

            def prefix(src, bufs, n, cut):
                for r in range((n - 1).bit_length()):
                    d, dst = 1 << r, bufs[r % 2]
                    nc.vector.tensor_copy(cut(dst, 0, d), cut(src, 0, d))
                    link(nc.vector.tensor_tensor(cut(dst, d, n), cut(src, d, n), cut(src, 0, n - d), ALU.add))
                    src = dst
                return src

            v.wait_ge(const_in, 16)
            nc.vector.tensor_copy(trib[:], cst[:, C_TRI:C_TRI + P])
            nc.vector.memset(zero[:].bitcast(F32), 0.0)
            nc.vector.memset(oneb[:], 1.0)
            nc.vector.tensor_tensor(gate[:], top[:, :, 0:K], top[:, :, 0:1].to_broadcast([P, NTILE, K]), ALU.subtract).then_inc(gd_ready, 1)
            link(nc.vector.tensor_copy(idxf[:], topi[:, :, 0:K]))
            iota_e = cst[:, C_IOTA:C_IOTA + E].rearrange("p (o e) -> p o e", o=1).to_broadcast([P, NTILE, E])
            for k in range(K):
                ins = nc.vector.tensor_tensor(hot[:, k], iota_e, idxf[:, :, k:k + 1].to_broadcast([P, NTILE, E]), ALU.is_equal)
            link(ins)
            nc.vector.tensor_tensor(cumA[:], hot[:, 0], hot[:, 1], ALU.add)
            link(nc.vector.tensor_tensor(cumB[:], hot[:, 2], hot[:, 3], ALU.add))
            nc.vector.tensor_tensor(anyb[:], cumA[:], cumB[:], ALU.add).then_inc(any_ready, 1)
            v.wait_ge(counted, 1)
            link(nc.vector.tensor_copy(tot[:], S[:].rearrange("p a (t e) -> p (a t) e", e=E)))
            cum = prefix(tot, (cumA, cumB), NTILE, lambda x, a, b: x[:, a:b])
            link(nc.vector.tensor_tensor(place[:], cum[:], tot[:], ALU.subtract))
            link(nc.vector.tensor_tensor(place[:], place[:], C[:].rearrange("p a (t e) -> p (a t) e", e=E), ALU.add))
            link(nc.vector.tensor_scalar(nti[:], cum[:, NTILE - 1], P - 1.0, None, ALU.add))
            link(nc.vector.tensor_scalar(nti[:], nti[:], 7, None, ALU.arith_shift_right))
            link(nc.vector.tensor_scalar(ntf[:], nti[:], 1.0, None, ALU.max))
            ends = prefix(ntf, (ca, cb), E, lambda x, a, b: x[:, a:b])
            link(nc.vector.tensor_tensor(base[:], ends[:], ntf[:], ALU.subtract))
            link(nc.vector.tensor_scalar(base[:], base[:], float(P), None, ALU.mult))
            link(nc.vector.tensor_copy(par[:, 0:1], ends[:, E - 1:E]))
            link(nc.vector.tensor_scalar(par[:, 1:2], par[:, 0:1], 1, None, ALU.bitwise_and))
            link(nc.vector.tensor_tensor(ends[:, E - 1:E], ends[:, E - 1:E], par[:, 1:2], ALU.add))
            nc.vector.memset(ctab[:], 0)
            iota_t = cst[:, C_IOTA:C_IOTA + XW].rearrange("p (t o) -> p t o", o=1).to_broadcast([P, XW, E])
            link(nc.vector.tensor_tensor(over[:], iota_t, ends[:].rearrange("p (o e) -> p o e", o=1).to_broadcast([P, XW, E]), ALU.is_ge))
            nc.vector.tensor_copy(ctab[:, 1:E + 1], ends[:])
            link(nc.vector.tensor_reduce(etf[:], over[:], AX_X, ALU.add))
            nc.vector.memset(etab[:], 0)
            link(nc.vector.tensor_scalar(etf[:], etf[:], E - 1.0, None, ALU.min))
            nc.vector.tensor_copy(etab[:, 1:XW + 1], etf[:])
            link(nc.vector.tensor_tensor(place[:], place[:], base[:].rearrange("p (o e) -> p o e", o=1).to_broadcast([P, NTILE, E]), ALU.add))
            for k in range(K):
                ins = nc.vector.tensor_tensor(hot[:, k], hot[:, k], place[:], ALU.mult)
            link(ins)
            for k in range(K):
                ins = nc.vector.tensor_reduce(slotf[:, :, k], hot[:, k], AX_X, ALU.add)
            link(ins)
            link(nc.vector.tensor_copy(sloti[:], slotf[:]))
            nc.vector.tensor_scalar(slots[:], slotf[:], float(P), None, ALU.add)
            link(nc.vector.tensor_scalar(tmpi[:], sloti[:], 7, None, ALU.arith_shift_right))
            link(nc.vector.tensor_copy(tilef[:], tmpi[:]))
            link(nc.vector.tensor_scalar(tmpi[:], sloti[:], P - 1, None, ALU.bitwise_and))
            link(nc.vector.tensor_copy(posf[:], tmpi[:]))
            v.wait_ge(ge_ready, 1)
            link(nc.vector.tensor_reduce(gs[:], gate[:], AX_X, ALU.add))
            link(nc.vector.reciprocal(gr[:], gs[:]))
            link(nc.vector.tensor_tensor(gate[:], gate[:], gr[:].rearrange("p (t o) -> p t o", o=1).to_broadcast([P, NTILE, K]), ALU.mult))
            v.sem_inc(sel_ready, 1)
            with v.Fori(0, NTILE) as i:
                wait_apart(v, listed, i + 1)
                for k in range(K):
                    nc.vector.tensor_scalar(selp[:, k], cst[:, C_IOTA:C_IOTA + P], posf[:, bass.ds(i, 1), k], None, ALU.is_equal)
                    ins = nc.vector.tensor_scalar(selt[:, k], cst[:, C_IOTA:C_IOTA + XW], tilef[:, bass.ds(i, 1), k],
                                                  cst[:, bass.ds(i + C_TOK, 1)], ALU.is_equal, ALU.mult)
                ins.then_inc(sel_ready, 1)
            v.wait_ge(listed, NTILE + 2)
            nc.vector.tensor_copy(ids[:], I[:, 0:XW])

            def lo_h(i):
                v.wait_ge(hh_done, i + 1)
                nc.vector.tensor_tensor(flatten(hTl), TP[:, 0], flatten(hTh).bitcast(F32), ALU.subtract).then_inc(hl_done, 1)

            def down(i, q, s):
                v.wait_ge(dn_done, i + 1)
                v.wait_ge(h0_in[s], q * 16 + 16)
                v.wait_ge(base_out[s], q * 16 + 16)
                nc.vector.tensor_tensor(outb[:, s], O[:], h0b[:, s], ALU.add).then_inc(base_ready, 1)

            def tile(i, q, s, first=False):
                v.wait_ge(silu_done, i + 1)
                nc.vector.tensor_tensor(ac[:], sl[:], S[:, 1], ALU.mult).then_inc(act_ready, 1)
                lo_h(i + 1)
                if not first:
                    down(i - 1, q if s else q - 1, 1 - s)
                v.wait_ge(ah_done, i + 1)
                nc.vector.tensor_tensor(flatten(aTl), TP[:, 1], flatten(aTh).bitcast(F32), ALU.subtract).then_inc(al_done, 1)

            lo_h(0)
            tile(0, 0, 0, first=True)
            tile(1, 0, 1)
            with v.Fori(1, NTILE // 2) as j:
                for s in range(2):
                    tile(v.snap(j * 2 + s), j, s)
            down(NTILE - 1, NTILE // 2 - 1, 1)

        @block.scalar
        def _(act):
            act.wait_ge(gd_ready, 1)
            nc.scalar.activation(gate[:], gate[:], ACT.Exp).then_inc(ge_ready, 1)

            def hi_h(i):
                act.wait_ge(t_done, i + 1)
                nc.scalar.copy(flatten(hTh), TP[:, 0]).then_inc(hh_done, 1)

            def tile(i):
                act.wait_ge(gu_done, i + 1)
                nc.scalar.activation(sl[:], S[:, 0], ACT.Silu).then_inc(silu_done, 1)
                hi_h(i + 1)
                act.wait_ge(at_done, i + 1)
                nc.scalar.copy(flatten(aTh), TP[:, 1]).then_inc(ah_done, 1)

            hi_h(0)
            with act.Fori(0, NTILE) as i:
                tile(i)

        @block.tensor
        def _(pe):
            mm = nc.tensor.matmul
            ident = cst[:, C_ID:C_ID + P]

            def mm3(out, ah, al, bh, bl, first, last):
                mm(out, ah, bh, start=first, stop=False)
                mm(out, ah, bl, start=False, stop=False)
                return mm(out, al, bh, start=False, stop=last)

            pe.wait_ge(const_in, 16)
            pe.wait_ge(any_ready, 1)
            flat = anyb[:].rearrange("p t e -> p (t e)")
            for a in range(2):
                mm(C[:, a], trib[:], flat[:, a * 512:(a + 1) * 512], start=True, stop=True)
                ins = mm(S[:, a], oneb[:], flat[:, a * 512:(a + 1) * 512], start=True, stop=True)
            ins.then_inc(counted, 1)
            pe.wait_ge(sel_ready, 1)
            mm(I[:, 0:XW], zero[:, 0:P], zero[:], start=True, stop=False).then_inc(listed, 1)
            with pe.Fori(0, NTILE) as i:
                pe.wait_ge(sel_ready, i + 2)
                for k in range(K):
                    ins = mm(I[:, 0:XW], selp[:, k], selt[:, k], start=False, stop=False)
                ins.then_inc(listed, 1)
            mm(I[:, 0:XW], zero[:, 0:P], zero[:], start=False, stop=True).then_inc(listed, 1)

            def transpose_h(i, q, s):
                pe.wait_ge(h_in[s], q * 16 + 16)
                for c in range(MC):
                    ins = nc.tensor.transpose(TP[:, 0, c * P:(c + 1) * P], hb[:, s, c * P:(c + 1) * P], ident)
                ins.then_inc(t_done, 1)

            def down(i):
                pe.wait_ge(al_done, i + 1)
                for c in range(MC):
                    ins = mm3(O[:], aTh[:, c], aTl[:, c], wh[:, 2, c], wl[:, 2, c], c == 0, c == MC - 1)
                ins.then_inc(dn_done, 1)

            def tile(i, q, s, first=False):
                pe.wait_ge(hl_done, i + 1)
                if first:
                    pe.wait_ge(stage_free, 3 * MC)
                for c in range(MC):
                    for w in range(2):
                        ins = mm3(S[:, w], hTh[:, c], hTl[:, c], wh[:, w, c], wl[:, w, c], c == 0, c == MC - 1)
                ins.then_inc(gu_done, 1)
                transpose_h(i + 1, q + s, 1 - s)
                if not first:
                    if s == 1 and isinstance(i, int):
                        pass
                    else:
                        pe.wait_ge(base_ready, i - 1)
                    down(i - 1)
                pe.wait_ge(act_ready, i + 1)
                for c in range(MC):
                    ins = nc.tensor.transpose(TP[:, 1, c * P:(c + 1) * P], ac[:, c * P:(c + 1) * P], ident)
                ins.then_inc(at_done, 1)

            transpose_h(0, 0, 0)
            tile(0, 0, 0, first=True)
            tile(1, 0, 1)
            with pe.Fori(1, NTILE // 2) as j:
                for s in range(2):
                    tile(pe.snap(j * 2 + s), j, s)
            pe.wait_ge(base_ready, NTILE - 1)
            down(NTILE - 1)


def experts(nc, w1, w2, const, h_d, y_d, ids, etab, ctab):
    with ExitStack() as ctx:
        def sb(name, shape, dt=F32):
            return ctx.enter_context(nc.sbuf_tensor(name, shape, dt))

        def sem(name):
            return ctx.enter_context(nc.semaphore(name))

        WC = (MC + FI // P) * M
        QC = WC // 3
        idn = sb("idn", [P, P])
        raww = sb("raww", [P, 2, WC])
        wh, wl = sb("weh", [P, 2, WC], F32R), sb("wel", [P, 2, WC], F32R)
        idx = sb("idx3", [P, 2], I32)
        xg = sb("xg", [P, 2, M])
        hTh, hTl = sb("hTh3", [P, MC, P], F32R), sb("hTl3", [P, MC, P], F32R)
        aTh, aTl = sb("aTh3", [P, FI], F32R), sb("aTl3", [P, FI], F32R)
        sl, ac = sb("sl3", [P, FI]), sb("ac3", [P, FI])
        yb = sb("yb", [P, 2, M])
        blank = sb("blank", [P, M])

        S = ctx.enter_context(nc.psum_tensor("S3", [P, 512], F32))
        TP = ctx.enter_context(nc.psum_tensor("TP3", [P, 2, 512], F32))
        O = ctx.enter_context(nc.psum_tensor("O3", [P, 512], F32))

        const_in = sem("const_in3")
        raw_in = [sem("raw_in0"), sem("raw_in1")]
        wh_ready, wl_ready = sem("wh_ready"), sem("wl_ready")
        idx_ready = sem("idx_ready")
        x_in = [sem("xg_in0"), sem("xg_in1")]
        t_done, hh_done, hl_done = sem("t_done3"), sem("hh_done3"), sem("hl_done3")
        gu_done, silu_done, act_ready = sem("gu_done3"), sem("silu_done3"), sem("act_ready3")
        at_done, ah_done, al_done = sem("at_done3"), sem("ah_done3"), sem("al_done3")
        dn_done, y_ready = sem("dn_done3"), sem("y_ready3")
        y_out = [sem("y_out0"), sem("y_out1")]

        block = ctx.enter_context(nc.Block())

        blank_ready, blank_out = sem("blank_ready"), sem("blank_out")
        y_stored, y_free = sem("y_stored"), sem("y_free")

        def total(eng):
            return eng.value_load(ctab[0:1, E:E + 1], min_val=4, max_val=XT)

        @block.sync
        def _(sp):
            sp.dma_start(idn[:], const[:, C_ID:C_ID + P]).then_inc(const_in, 16)
            sp.sem_inc(y_free, 2)
            y_t = y_d.rearrange("(t p) m -> t p m", p=P)

            def store(n, s):
                sp.wait_ge(y_ready, n + 1)
                sp.dma_start(y_t[n], yb[:, s]).then_inc(y_stored, 16)
                sp.wait_ge(y_stored, n * 16 + 16)
                sp.sem_inc(y_free, 1)

            store(0, 0)
            pairs = sp.snap(total(sp) // 2)
            with sp.Fori(0, pairs) as j:
                store(sp.snap(j * 2 + 1), 1)
                store(sp.snap(j * 2 + 2), 0)

        @block.gpsimd
        def _(pool):
            h_rows = h_d.rearrange("b t m -> (b t) m")

            def gather(t, s):
                wait_apart(pool, t_done, t + 1)
                nc.gpsimd.tensor_copy(idx[:, s:s + 1], ids[:, bass.ds(t, 1)]).then_inc(idx_ready, 1)
                wait_apart(pool, idx_ready, t + 1)
                nc.gpsimd.indirect_dma_start(xg[:, s], None, h_rows, bass.IndirectOffsetOnAxis(ap=idx[:, s:s + 1], axis=0)).then_inc(x_in[s], 16)

            gather(0, 0)
            tiles = pool.snap(total(pool))
            y_t = y_d.rearrange("(t p) m -> t p m", p=P)
            pool.wait_ge(blank_ready, 1)
            with pool.Fori(0, XT - tiles) as r:
                pool.dma_start(y_t[nc.s_assert_within(XT - r, 1, XT)], blank[:]).then_inc(blank_out, 16)
            pairs = pool.snap(tiles // 2)
            with pool.Fori(0, pairs) as j:
                gather(pool.snap(j * 2 + 1), 1)
                gather(pool.snap(j * 2 + 2), 0)
            with pool.Fori(0, XT - tiles) as r:
                pool.wait_ge(blank_out, r * 16 + 16)

        def third(r):
            return bass.ds(nc.s_assert_within(r * QC, 0, 2 * QC, skip_runtime_bounds_check_because="it stands under If r < 3"), QC)

        @block.scalar
        def _(act):
            def load(e, s):
                act.dma_start(raww[:, s, 0:MC * M].rearrange("p (c f) -> p c f", c=MC),
                              w1[e].rearrange("(c p) f -> p c f", p=P)).then_inc(raw_in[s], 16)
                act.dma_start(raww[:, s, MC * M:WC].rearrange("p (c f) -> p c f", c=FI // P),
                              w2[e].rearrange("(c p) f -> p c f", p=P)).then_inc(raw_in[s], 16)

            def hi_h(t):
                act.wait_ge(t_done, t + 1 + 2)
                nc.scalar.copy(flatten(hTh), TP[:, 0]).then_inc(hh_done, 1)

            def result(n):
                wait_apart(act, dn_done, n + 1)
                act.wait_ge(y_free, n + 1)
                nc.scalar.copy(yb[:, n % 2, :], O[:]).then_inc(y_ready, 1)

            load(0, 0)
            load(1, 1)
            act.wait_ge(raw_in[0], 32)
            for r in range(3):
                nc.scalar.copy(wh[:, 0, r * QC:(r + 1) * QC], raww[:, 0, r * QC:(r + 1) * QC]).then_inc(wh_ready, 1)
            hi_h(0)
            with act.Fori(0, E // 2) as j:
                for s in range(2):
                    e = act.snap(j * 2 + s)
                    act.wait_ge(wl_ready, e * 3 + 3)
                    load((e + 2) % E, s)
                    t0 = act.value_load(ctab[0:1, bass.ds(e, 1)], min_val=0, max_val=XT)
                    t1 = act.value_load(ctab[0:1, bass.ds(e + 1, 1)], min_val=1, max_val=XT)
                    wait_apart(act, raw_in[1 - s], j * 32 + 32 * (s + 1))
                    with act.Fori(0, t1 - t0) as r:
                        t = act.snap(t0 + r)
                        act.wait_ge(gu_done, t + 1)
                        nc.scalar.activation(sl[:], S[:, 0:FI], ACT.Silu).then_inc(silu_done, 1)
                        hi_h(t + 1)
                        result(t)
                        act.wait_ge(at_done, t + 1)
                        nc.scalar.copy(aTh[:], TP[:, 1, 0:FI]).then_inc(ah_done, 1)
                        with act.If(r < 3):
                            nc.scalar.copy(wh[:, 1 - s, third(r)], raww[:, 1 - s, third(r)]).then_inc(wh_ready, 1)
                    for m in (1, 2):
                        with act.If(t1 < t0 + (m + 1)):
                            wait_apart(act, dn_done, t0 + 1)
                            nc.scalar.copy(wh[:, 1 - s, m * QC:(m + 1) * QC], raww[:, 1 - s, m * QC:(m + 1) * QC]).then_inc(wh_ready, 1)
            result(total(act))
            for s in range(2):
                act.wait_ge(raw_in[s], 32 * (E // 2 + 1))

        @block.vector
        def _(v):
            nc.vector.memset(blank[:], 0.0).then_inc(blank_ready, 1)
            nc.vector.memset(aTh[:].bitcast(F32), 0.0)
            nc.vector.memset(aTl[:].bitcast(F32), 0.0).then_inc(al_done, 1)

            def split_lo(s, at, count):
                wait_apart(v, wh_ready, count)
                nc.vector.tensor_tensor(wl[:, s, at], raww[:, s, at], wh[:, s, at].bitcast(F32), ALU.subtract).then_inc(wl_ready, 1)

            def lo_h(t):
                v.wait_ge(hh_done, t + 1)
                nc.vector.tensor_tensor(flatten(hTl), TP[:, 0], flatten(hTh).bitcast(F32), ALU.subtract).then_inc(hl_done, 1)

            for r in range(3):
                split_lo(0, slice(r * QC, (r + 1) * QC), r + 1)
            lo_h(0)
            with v.Fori(0, E // 2) as j:
                for s in range(2):
                    e = v.snap(j * 2 + s)
                    t0 = v.value_load(ctab[0:1, bass.ds(e, 1)], min_val=0, max_val=XT)
                    t1 = v.value_load(ctab[0:1, bass.ds(e + 1, 1)], min_val=1, max_val=XT)
                    with v.Fori(0, t1 - t0) as r:
                        t = v.snap(t0 + r)
                        v.wait_ge(silu_done, t + 1)
                        nc.vector.tensor_tensor(ac[:], sl[:], S[:, FI:2 * FI], ALU.mult).then_inc(act_ready, 1)
                        lo_h(t + 1)
                        v.wait_ge(ah_done, t + 1)
                        nc.vector.tensor_tensor(aTl[:], TP[:, 1, 0:FI], aTh[:].bitcast(F32), ALU.subtract).then_inc(al_done, 1)
                        with v.If(r < 3):
                            split_lo(1 - s, third(r), e * 3 + 3 + r + 1)
                    for m in (1, 2):
                        with v.If(t1 < t0 + (m + 1)):
                            split_lo(1 - s, slice(m * QC, (m + 1) * QC), e * 3 + 3 + m + 1)

        @block.tensor
        def _(pe):
            mm = nc.tensor.matmul
            whf, wlf = (w[:].rearrange("p s c -> p (s c)") for w in (wh, wl))

            def mm3(out, ah, al, bh, bl, first, last):
                mm(out, ah, bh, start=first, stop=False)
                mm(out, ah, bl, start=False, stop=False)
                return mm(out, al, bh, start=False, stop=last)

            def expert_of(t):
                return pe.value_load(etab[0:1, bass.ds(t + 1, 1)], min_val=0, max_val=E - 1)

            def transpose_x(t, q, s):
                pe.wait_ge(x_in[s], q * 16 + 16)
                for c in range(MC):
                    ins = nc.tensor.transpose(TP[:, 0, c * P:(c + 1) * P], xg[:, s, c * P:(c + 1) * P], idn[:])
                ins.then_inc(t_done, 1)

            def down(t, place):
                pe.wait_ge(al_done, t + 2)
                for c in range(FI // P):
                    at = bass.ds(place * WC + (MC + c) * M, M)
                    ins = mm3(O[:], aTh[:, c * P:(c + 1) * P], aTl[:, c * P:(c + 1) * P], whf[:, at], wlf[:, at], c == 0, c == FI // P - 1)
                ins.then_inc(dn_done, 1)

            def tile(t, q, s, first=False):
                e = expert_of(t)
                place = pe.snap(e % 2)
                before = None if first else pe.snap(expert_of(t - 1) % 2)
                pe.wait_ge(wl_ready, e * 3 + 3)
                pe.wait_ge(hl_done, t + 1)
                for c in range(MC):
                    at = bass.ds(place * WC + c * M, M)
                    ins = mm3(S[:], hTh[:, c], hTl[:, c], whf[:, at], wlf[:, at], c == 0, c == MC - 1)
                ins.then_inc(gu_done, 1)
                transpose_x(t + 1, q + s, 1 - s)
                if not first:
                    pe.wait_ge(y_ready, t)
                    down(t - 1, before)
                pe.wait_ge(act_ready, t + 1)
                for c in range(FI // P):
                    ins = nc.tensor.transpose(TP[:, 1, c * P:(c + 1) * P], ac[:, c * P:(c + 1) * P], idn[:])
                ins.then_inc(at_done, 1)

            pe.sem_inc(t_done, 2)
            pe.wait_ge(const_in, 16)
            transpose_x(0, 0, 0)
            pe.wait_ge(wl_ready, 3)
            down(-1, 0)
            tile(0, 0, 0, first=True)
            tile(1, 0, 1)
            pairs = pe.snap(total(pe) // 2)
            with pe.Fori(1, pairs) as j:
                for s in range(2):
                    tile(pe.snap(j * 2 + s), j, s)
            n = pe.snap(pairs * 2)
            before = pe.snap(expert_of(n - 1) % 2)
            pe.wait_ge(y_ready, n)
            down(n - 1, before)


def combine(nc, base_d, x2_d, y_d, out, slots, gate):
    with ExitStack() as ctx:
        def sb(name, shape, dt=F32):
            return ctx.enter_context(nc.sbuf_tensor(name, shape, dt))

        def sem(name):
            return ctx.enter_context(nc.semaphore(name))

        idx = sb("idx4", [P, 2, K], I32)
        yg = sb("yg", [P, 2, K, M])
        acc, x2, ob = sb("acc4", [P, 2, M]), sb("x24", [P, 2, M]), sb("ob4", [P, 2, M])
        gt = sb("gt4", [P, 2, K])
        stat, mv = sb("stat4", [P, 2, 6]), sb("mv4", [P, 2, 2])
        ve, std, rstd = sb("ve4", [P, 2]), sb("std4", [P, 2]), sb("rstd4", [P, 2])

        b_in, x_in = [sem("b_in0"), sem("b_in1")], [sem("x2_in0"), sem("x2_in1")]
        y_in = [sem("y_in0"), sem("y_in1")]
        idx_ready = sem("idx_ready4")
        step = sem("step4")
        summed = sem("summed")
        var_ready, std_ready = sem("var_ready4"), sem("std_ready4")
        out_ready = sem("out_ready4")
        out_stored = [sem("out_stored0"), sem("out_stored1")]

        block = ctx.enter_context(nc.Block())
        HALVES = NTILE // 2

        @block.sync
        def _(sp):
            base_t = base_d.rearrange("(t p) m -> t p m", p=P)
            x2_t = x2_d.rearrange("b (t p) m -> (b t) p m", p=P)
            out_t = out.rearrange("b (t p) m -> (b t) p m", p=P)
            for s in range(2):
                sp.sem_inc(out_stored[s], 16)
                sp.dma_start(acc[:, s], base_t[s]).then_inc(b_in[s], 16)
                sp.dma_start(x2[:, s], x2_t[s]).then_inc(x_in[s], 16)
            with sp.Fori(0, HALVES) as j:
                for s in range(2):
                    i = sp.snap(j * 2 + s)
                    nxt = sp.snap((i + 2) % NTILE)
                    sp.wait_ge(out_ready, i + 1)
                    sp.dma_start(out_t[i], ob[:, s]).then_inc(out_stored[s], 16)
                    sp.dma_start(acc[:, s], base_t[nxt]).then_inc(b_in[s], 16)
                    sp.dma_start(x2[:, s], x2_t[nxt]).then_inc(x_in[s], 16)
            for s in range(2):
                for x, n in ((out_stored, 1), (b_in, 1), (x_in, 1)):
                    sp.wait_ge(x[s], 16 * (HALVES + n))

        @block.gpsimd
        def _(pool):
            y_rows = y_d
            with pool.Fori(0, HALVES) as j:
                for s in range(2):
                    i = pool.snap(j * 2 + s)
                    wait_apart(pool, summed, i + 1)
                    nc.gpsimd.tensor_copy(idx[:, s, :], slots[:, bass.ds(i, 1), :]).then_inc(idx_ready, 1)
                    wait_apart(pool, idx_ready, i + 1)
                    for k in range(K):
                        nc.gpsimd.indirect_dma_start(yg[:, s, k], None, y_rows,
                                                     bass.IndirectOffsetOnAxis(ap=idx[:, s, k:k + 1], axis=0)).then_inc(y_in[s], 16)

        @block.vector
        def _(v):
            v.sem_inc(summed, 2)
            STEPS = 9
            with v.Fori(0, HALVES) as j:
                for s in range(2):
                    i = v.snap(j * 2 + s)
                    c = v.snap(i * STEPS)
                    done = [0]

                    def link(ins):
                        done[0] += 1
                        ins.then_inc(step, 1)
                        wait_apart(v, step, c + done[0])

                    wait_apart(v, b_in[s], j * 16 + 16)
                    v.wait_ge(y_in[s], j * 64 + 64)
                    link(nc.vector.tensor_copy(gt[:, s, :], gate[:, bass.ds(i, 1), :]))
                    for k in range(K):
                        link(nc.vector.scalar_tensor_tensor(out=acc[:, s], in0=yg[:, s, k], scalar=gt[:, s, k:k + 1], in1=acc[:, s],
                                                            op0=ALU.mult, op1=ALU.add))
                    link(nc.vector.bn_stats(stat[:, s], acc[:, s]))
                    link(nc.vector.bn_aggr(mv[:, s], stat[:, s]))
                    nc.vector.tensor_scalar(ve[:, s:s + 1], mv[:, s, 1:2], LN_EPS, None, ALU.add).then_inc(var_ready, 1)
                    v.wait_ge(std_ready, i + 1)
                    link(nc.vector.reciprocal(rstd[:, s:s + 1], std[:, s:s + 1]))
                    v.wait_ge(out_stored[s], j * 16 + 16)
                    link(nc.vector.tensor_scalar(ob[:, s], acc[:, s], mv[:, s, 0:1], rstd[:, s:s + 1], ALU.subtract, ALU.mult))
                    v.wait_ge(x_in[s], j * 16 + 16)
                    nc.vector.tensor_tensor(ob[:, s], ob[:, s], x2[:, s], ALU.add).then_inc(out_ready, 1)
                    v.sem_inc(summed, 1)
                    assert done[0] == STEPS

        @block.scalar
        def _(act):
            with act.Fori(0, HALVES) as j:
                for s in range(2):
                    act.wait_ge(var_ready, j * 2 + s + 1)
                    nc.scalar.activation(std[:, s:s + 1], ve[:, s:s + 1], ACT.Sqrt).then_inc(std_ready, 1)


def build(nc, x, w_aq, w_ak, w_av, w_ao, norm_w, router_w, w1, w2, sg, su, sd, const, out):
    x2_d = nc.dram_tensor("x2_d", (B, T, M), F32).ap()
    h0_d = nc.dram_tensor("h0_d", (B, T, M), F32).ap()
    h_d = nc.dram_tensor("h_d", (B, T, M), F32).ap()
    base_d = nc.dram_tensor("base_d", (NTOK, M), F32).ap()
    y_d = nc.dram_tensor("y_d", ((XT + 1) * P, M), F32).ap()
    with ExitStack() as logits:
        top = logits.enter_context(nc.sbuf_tensor("top", [P, NTILE, 8], F32))
        topi = logits.enter_context(nc.sbuf_tensor("topi", [P, NTILE, 8], U32))
        attention(nc, x, w_aq, w_ak, w_av, w_ao, norm_w, router_w, const, x2_d, h0_d, h_d, top, topi)
        with ExitStack() as ctx:
            def keep(name, shape, dt):
                return ctx.enter_context(nc.sbuf_tensor(name, shape, dt))

            slots = keep("slots", [P, NTILE, K], I32)
            gate = keep("gate", [P, NTILE, K], F32)
            ids = keep("ids", [P, XW], I32)
            etab = keep("etab", [P, XW + 1], I32)
            ctab = keep("ctab", [P, E + 1], I32)
            dispatch(nc, sg, su, sd, const, h0_d, h_d, base_d, top, topi, slots, gate, ids, etab, ctab)
            experts(nc, w1, w2, const, h_d, y_d, ids, etab, ctab)
            combine(nc, base_d, x2_d, y_d, out, slots, gate)


_INS = ['L0_attn_x', 'L0_attn_w_aq', 'L0_attn_w_ak', 'L0_attn_w_av', 'L0_attn_w_ao', 'L0_ffn_norm_w', 'L0_ffn_router_w',
        'L0_ffn_w1', 'L0_ffn_w2', 'L0_ffn_sg', 'L0_ffn_su', 'L0_ffn_sd']


def _constants():
    import numpy as np

    c = np.zeros((P, C_W), np.float32)
    c[:, C_ID:C_ID + P] = np.eye(P)
    i = np.arange(P)
    c[:, C_MASK:C_MASK + P] = np.where(i[:, None] < i[None, :], MASKED, 0.0)
    c[:, C_TRI:C_TRI + P] = i[:, None] < i[None, :]
    freq = np.power(np.float32(10000.0), -np.arange(HALF, dtype=np.float32) / np.float32(HALF)).astype(np.float32)
    angle = (np.arange(T, dtype=np.float32)[:, None] * freq[None, :]).astype(np.float32).reshape(NT, P, HALF)
    angle = angle.transpose(1, 0, 2).reshape(P, NT * HALF)
    mult = np.float32(D ** -0.25)
    c[:, C_COS:C_COS + NT * HALF] = np.cos(angle) * mult
    c[:, C_SIN:C_SIN + NT * HALF] = np.sin(angle) * mult
    c[:, C_NSIN:C_NSIN + NT * HALF] = -np.sin(angle) * mult
    c[:, C_IOTA:C_IOTA + C_TOK - C_IOTA] = np.arange(C_TOK - C_IOTA)
    c[:, C_TOK:C_TOK + NTILE] = np.arange(NTILE)[None, :] * P + i[:, None]
    return c


def kernel(**inputs):
    import numpy as _np
    import concourse.bacc as _bacc
    from concourse import mybir as _mybir
    from concourse.bass_utils import run_bass_kernel_spmd as _run

    nc = _bacc.Bacc("TRN2", target_bir_lowering=False, num_devices=1)
    arrays, args = {}, []
    named = [(name, _np.ascontiguousarray(inputs[name])) for name in _INS] + [("constants", _constants())]
    for name, a in named:
        arrays[f"in_{name}_dram"] = a
        args.append(nc.dram_tensor(f"in_{name}_dram", a.shape, _mybir.dt.from_np(a.dtype), kind="ExternalInput").ap())
    args.append(nc.dram_tensor("out_0_dram", (B, T, M), _mybir.dt.float32, kind="ExternalOutput").ap())
    build(nc, *args)
    r = _run(nc, [arrays], core_ids=[0])
    return r.results[0]["out_0_dram"]
```

```python
from contextlib import ExitStack

import concourse.bass as bass
from concourse import mybir

ALU = mybir.AluOpType
ACT = mybir.ActivationFunctionType
AX_X = mybir.AxisListType.X
F32 = mybir.dt.float32
F32R = mybir.dt.float32r
BF16 = mybir.dt.bfloat16
I32 = mybir.dt.int32
U32 = mybir.dt.uint32

P = 128
B, T, M = 4, 1024, 512
G, H, D = 4, 4, 128
MC = M // P
NT = T // P
NTOK = B * T
NTILE = NTOK // P
E, K = 32, 4
FI = 256
FS = 512
QW = H * D
PW = QW + 2 * D
RW = QW + D
HALF = D // 2
LN_EPS, RMS_EPS = 1e-5, 1e-6
MASKED = -1e30
XT = NTOK * K // P + E
WC = (MC + FI // P) * M
XW = XT + 2

IB = 2
NIB = NT // IB
BLOCKS = [(a, NIB - 1 - a) for a in reversed(range(NIB // 2))]
UNITS = [(ib, h) for blocks in BLOCKS for h in range(H) for ib in blocks]
PAIRS = [(u, jp) for u, (ib, h) in enumerate(UNITS) for jp in range(ib + 1)]
NPAIR = len(PAIRS)
PAIR_OF = {p: n for n, p in enumerate(PAIRS)}

SG = NT + 2 * len(UNITS)
TG = 2 * NT + NPAIR
MG = len(UNITS) + NT
TB = NT + G * TG + NT
MB = G * MG + NT

C_ID, C_COS, C_SIN, C_MASK, C_TRI, C_IOTA, C_TOK = 0, 128, 640, 1152, 1280, 1408, 1600
C_W = 1632


def wait_apart(eng, sem, value):
    value = eng.to_reg(value)
    eng.wait_ge(sem, 1)
    eng.wait_ge(sem, value)


def flatten(t):
    return t[:].rearrange("p c n -> p (c n)")


HALFU = len(UNITS) // 2
PROJECT_AT = {HALFU + n: [IB * BLOCKS[0][n] + a for a in range(IB)] for n in range(2)}
PROJECT_LAST = [IB * ib + a for ib in BLOCKS[1] for a in range(IB)]

OUTPUTS = [x for u in range(len(UNITS)) for x in [("r", t) for t in PROJECT_AT.get(u, [])] + [("o", u)]]
OUTPUTS += [("r", t) for t in PROJECT_LAST]
PROJECTED = [n for kind, n in OUTPUTS if kind == "r"]


def load_expert(eng, raww, s, w1, w2, loaded):
    eng.dma_start(raww[:, s, 0:MC * M].rearrange("p (c f) -> p c f", c=MC), w1.rearrange("(c p) f -> p c f", p=P)).then_inc(loaded, 16)
    eng.dma_start(raww[:, s, MC * M:WC].rearrange("p (c f) -> p c f", c=FI // P), w2.rearrange("(c p) f -> p c f", p=P)).then_inc(loaded, 16)


def attention(nc, x, w_aq, w_ak, w_av, w_ao, norm_w, router_w, const, x2_d, h_d, topi, coef):
    with ExitStack() as ctx:
        def sb(name, shape, dt=F32):
            return ctx.enter_context(nc.sbuf_tensor(name, shape, dt))

        def sem(name):
            return ctx.enter_context(nc.semaphore(name))

        cst = sb("cst", [P, C_MASK])
        xTh, xTl = sb("xTh", [P, MC, T], F32R), sb("xTl", [P, MC, T], F32R)
        qTh, qTl = sb("qTh", [P, H, T], F32R), sb("qTl", [P, H, T], F32R)
        kTh, kTl = sb("kTh", [P, T], F32R), sb("kTl", [P, T], F32R)
        vh, vl = sb("vh", [P, NT, D], F32R), sb("vl", [P, NT, D], F32R)
        wph, wpl = sb("wph", [P, MC, PW], F32R), sb("wpl", [P, MC, PW], F32R)
        woh, wol = sb("woh", [P, H, M], F32R), sb("wol", [P, H, M], F32R)
        stage = sb("stage", [P, 2, M])
        prob = sb("prob", [P, 2, IB, T])
        pth, ptl = sb("pth", [P, 2, M], F32R), sb("ptl", [P, 2, M], F32R)
        oTh, oTl = sb("oTh", [P, 2, H, IB * P], F32R), sb("oTl", [P, 2, H, IB * P], F32R)
        racc = sb("racc", [P, NT, M])
        work = sb("work", [P, NT, M])
        lgt = sb("lgt", [P, 2, E])
        rwTh, rwTl = sb("rwTh", [P, MC, E], F32R), sb("rwTl", [P, MC, E], F32R)
        nwb = sb("nwb", [P, M])
        idb, mskb = sb("idb", [P, P], BF16), sb("mskb", [P, P], BF16)
        stat = sb("stat", [P, NT, 6])
        mv = sb("mv", [P, NT, 2])
        vareps, std, rstd = sb("vareps", [P, NT]), sb("std", [P, NT]), sb("rstd", [P, NT])
        ssq = sb("ssq", [P, NT])
        onorm = sb("onorm", [P, IB * P])
        negmax, rsum, rinv = sb("negmax", [P, 4]), sb("rsum", [P, 4]), sb("rinv", [P, 4])
        top8, idx8 = sb("top8", [P, NT, 8]), sb("idx8", [P, NT, 8], U32)

        S = ctx.enter_context(nc.psum_tensor("S", [P, 2, 1024], F32))
        TP = ctx.enter_context(nc.psum_tensor("TP", [P, 2, 512], F32))
        O = ctx.enter_context(nc.psum_tensor("O", [P, 2, 512], F32))

        rw, mask = racc[0:E, 0], racc[:, 1, 0:P]
        flat = work[:].rearrange("p t m -> p (t m)")
        short = flat[:, 0:2 * IB * (T // 2)].rearrange("p (n a t) -> p n a t", n=2, a=IB)
        raw = [flat[:, i * PW:(i + 1) * PW] for i in range(2)]
        t1 = [flat[:, 2 * PW + i * RW:2 * PW + (i + 1) * RW] for i in range(2)]
        t2 = [flat[:, 2 * PW + (2 + i) * RW:2 * PW + (3 + i) * RW] for i in range(2)]
        xin = prob[:].rearrange("p a b t -> p (a b t)").rearrange("p (t m) -> p t m", m=M)
        ident = cst[:, C_ID:C_ID + P]
        cos = cst[:, C_COS:C_COS + NT * HALF].rearrange("p (t c) -> p t c", t=NT)
        sin = cst[:, C_SIN:C_SIN + NT * HALF].rearrange("p (t c) -> p t c", t=NT)

        def probs(u, a):
            if u == 0:
                return prob[:, 1, a]
            return (short if UNITS[u][0] < NIB // 2 else prob[:])[:, u // 2 % 2, a]

        def bank(kind, n):
            return O[:, OUTPUTS.index((kind, n)) % 2]

        def slot(parts, u):
            ib, h = UNITS[u]
            return parts[:, ib // (NIB // 2), h]

        const_in = sem("const_in")
        x_in = sem("x_in")
        stored = sem("stored")
        staged = [sem("staged0"), sem("staged1")]
        stage_free = sem("stage_free")
        w_hi = sem("w_hi")
        cast_ready = sem("cast_ready")
        rwT_ps, rwT_sb = sem("rwT_ps"), sem("rwT_sb")
        var_ready, std_ready = sem("var_ready"), sem("std_ready")
        dve = sem("dve")
        xln_ready = sem("xln_ready")
        s_done = sem("s_done")
        s_read = sem("s_read")
        turned = sem("turned")
        crossed = sem("crossed")
        tp_done, tp_hi, tp_lo = sem("tp_done"), sem("tp_hi"), sem("tp_lo")
        max_ready, rinv_ready = sem("max_ready"), sem("rinv_ready")
        over_ready = sem("over_ready")
        pv_done = sem("pv_done")
        o_hi = sem("o_hi")
        o_split = sem("o_split")
        o_free = sem("o_free")
        r_done = sem("r_done")
        lg_done = sem("lg_done")
        h_ready = sem("h_ready")
        out_ready = sem("out_ready")
        placed = sem("placed")
        sq_ready, sq_done = sem("sq_ready"), sem("sq_done")

        block = ctx.enter_context(nc.Block())

        @block.sync
        def _(sp):
            sp.dma_start(cst[:], const[:, 0:C_MASK]).then_inc(const_in, 16)
            sp.dma_start(mask, const[:, C_MASK:C_MASK + P]).then_inc(const_in, 16)
            sp.dma_start(rw, router_w).then_inc(const_in, 16)
            sp.dma_start(nwb[:], norm_w.rearrange("(a m) -> a m", a=1).to_broadcast([P, M])).then_inc(const_in, 16)

            def load_out(it, g):
                for h in range(H):
                    sp.wait_ge(stage_free, it * 10 + 6 + h + 1)
                    sp.dma_start(stage[:, h % 2], w_ao[g, h]).then_inc(staged[h % 2], 16)

            def load_proj(free, g, chunks=range(MC + 2)):
                for n in chunks:
                    sp.wait_ge(stage_free, free + n + 1)
                    if n < MC:
                        dst = stage[:, n % 2].rearrange("p (h d) -> p h d", h=H)
                        src = w_aq[g, :, n * P:(n + 1) * P, :].rearrange("h p d -> p h d")
                    else:
                        dst = stage[:, n % 2].rearrange("p (c d) -> p c d", c=MC)
                        src = (w_ak if n == MC else w_av)[g].rearrange("(c p) d -> p c d", p=P)
                    sp.dma_start(dst, src).then_inc(staged[n % 2], 16)

            load_proj(0, 0, range(2))
            sp.dma_start(xin, x[0].rearrange("(t p) m -> p t m", p=P)).then_inc(x_in, 16)
            load_proj(0, 0, range(2, MC + 2))
            with sp.Fori(0, B) as b:
                with sp.Fori(0, G) as g:
                    it = sp.snap(b * G + g)
                    load_out(it, g)
                    load_proj(it * 10 + 10, (g + 1) % G)
                sp.wait_ge(tp_done, b * TB + (NT + G * TG))
                sp.dma_start(xin, x[b].rearrange("(t p) m -> p t m", p=P)).then_inc(x_in, 16)
                sp.wait_ge(out_ready, b * 2 + 1)
                sp.dma_start(xin, x[(b + 1) % B].rearrange("(t p) m -> p t m", p=P)).then_inc(x_in, 16)
                sp.dma_start(x2_d[b].rearrange("(t p) m -> p t m", p=P), racc[:]).then_inc(stored, 16)
                sp.wait_ge(h_ready, b * NT + NT)
                sp.dma_start(h_d[b].rearrange("(t p) m -> p t m", p=P), work[:]).then_inc(stored, 16)
            sp.wait_ge(x_in, 16 * (2 * B + 1))
            sp.wait_ge(stored, 32 * B + 32)

        @block.gpsimd
        def _(pool):
            pool.sem_inc(stage_free, 2)
            pool.sem_inc(o_split, 1)

            def split(hi, lo, n, base, used):
                src = stage[:, n % 2]
                if len(hi.shape) == 3:
                    src = src.rearrange("p (c d) -> p c d", c=hi.shape[1])
                wait_apart(pool, staged[n % 2], used)
                nc.gpsimd.tensor_scalar(hi, src, 1.0, 1.0, ALU.mult, ALU.mult).then_inc(w_hi, 1)
                pool.wait_ge(w_hi, base + 1)
                nc.gpsimd.tensor_tensor(lo, src, hi.bitcast(F32), ALU.subtract).then_inc(stage_free, 1)

            def split_proj(n, base, dma):
                cols = (n, slice(0, QW)) if n < MC else (slice(0, MC), slice(QW + (n - MC) * D, QW + (n - MC + 1) * D))
                split(wph[:, cols[0], cols[1]], wpl[:, cols[0], cols[1]], n, base + n, dma + 16 * (n // 2 + 1))

            for n in range(MC + 2):
                split_proj(n, 0, 0)
            with pool.Fori(0, B) as b:
                with pool.Fori(0, G) as g:
                    it = pool.snap(b * G + g)
                    for t in range(NT):
                        pool.wait_ge(s_read, it * SG + t + 1 + 2)
                        pool.wait_ge(const_in, 64)
                        if t >= 2:
                            pool.wait_ge(turned, it * NT + t - 1)
                        src = raw[t % 2][:, 0:RW].rearrange("p (h s c) -> p h s c", s=2, c=HALF)
                        dst = t2[t % 2].rearrange("p (h s c) -> p h s c", s=2, c=HALF)
                        tab = sin[:, t:t + 1, :].to_broadcast([P, H + 1, HALF])
                        nc.gpsimd.tensor_tensor(dst[:, :, 0, :], src[:, :, 1, :], tab, ALU.mult)
                        nc.gpsimd.tensor_tensor(dst[:, :, 1, :], src[:, :, 0, :], tab, ALU.mult).then_inc(crossed, 1)
                    for u, (ib, h) in enumerate(UNITS):
                        if h == 0:
                            n = IB * (u % 2 + 1) if u >= HALFU else 0
                            pool.wait_ge(r_done, it * NT + n + 1)
                        wait_apart(pool, o_free, b * MB + g * MG + (OUTPUTS.index(("o", u)) + 1 + 2))
                        nc.gpsimd.tensor_scalar(slot(oTh, u), onorm[:], 1.0, 1.0, ALU.mult, ALU.mult).then_inc(o_hi, 1)
                        pool.wait_ge(o_hi, it * len(UNITS) + u + 1)
                        nc.gpsimd.tensor_tensor(slot(oTl, u), onorm[:], slot(oTh, u).bitcast(F32), ALU.subtract).then_inc(o_split, 1)
                        for n in {1: (0,), 3: (1, 2), 5: (3,)}.get(u, ()):
                            split(woh[:, n], wol[:, n], n, it * 10 + 6 + n, it * 80 + 48 + 16 * (n // 2 + 1))
                        if u == 7:
                            pool.wait_ge(s_done, it * SG + NT)
                        for n in {7: (0,), 9: (1,), 11: (2, 3), 13: (4,), 15: (5,)}.get(u, ()):
                            split_proj(n, it * 10 + 10, it * 80 + 80)

        @block.vector
        def _(v):
            v.sem_inc(tp_lo, 2)
            v.sem_inc(o_free, 2)
            v.sem_inc(stored, 32)
            v.wait_ge(const_in, 64)
            nc.vector.tensor_copy(idb[:], ident)
            nc.vector.tensor_copy(mskb[:], mask).then_inc(cast_ready, 1)
            v.wait_ge(rwT_ps, 1)
            rwT = TP[:, 0, 0:MC * E].rearrange("p (c e) -> p c e", c=MC)
            nc.vector.tensor_copy(rwTh[:], rwT).then_inc(rwT_sb, 1)
            v.wait_ge(rwT_sb, 1)
            nc.vector.tensor_tensor(rwTl[:], rwT, rwTh[:].bitcast(F32), ALU.subtract).then_inc(rwT_sb, 1)

            GD = NT * 3
            DVB = (3 * 2 - 1) * NT + 4 + 1 + NT + NT + 1 + 1 + G * GD

            def router(t, b, base, k):
                n = G * MG + t
                v.wait_ge(lg_done, b * NT + t + 1)
                if t >= 2:
                    v.wait_ge(placed, b * NT + t - 1)
                nc.vector.tensor_copy(lgt[:, t % 2], O[:, n % 2, 0:E]).then_inc(o_free, 1)
                wait_apart(v, o_free, b * MB + (n + 1 + 2))
                nc.vector.max(top8[:, t], lgt[:, t % 2]).then_inc(dve, 1)
                wait_apart(v, dve, base + (k + 1))
                nc.vector.max_index(idx8[:, t], top8[:, t], lgt[:, t % 2]).then_inc(placed, 1)
                return k + 1

            def link(ins, base, k):
                ins.then_inc(dve, 1)
                v.wait_ge(dve, base + (k + 1))
                return k + 1

            def stats(src_of, base, k, halves=False):
                if not halves:
                    for t in range(NT):
                        nc.vector.bn_stats(stat[:, t], src_of(t)).then_inc(dve, 1)
                    k += NT
                wait_apart(v, dve, base + k)
                for t in range(NT):
                    nc.vector.bn_aggr(mv[:, t], stat[:, t]).then_inc(dve, 1)
                k += NT
                v.wait_ge(dve, base + k)
                return k

            def root(src, eps, scale, base, k, roots):
                nc.vector.tensor_scalar(vareps[:], src, scale, eps, ALU.mult, ALU.add).then_inc(var_ready, 1)
                v.wait_ge(std_ready, roots)
                return link(nc.vector.reciprocal(rstd[:], std[:]), base, k)

            def center(t, src, dst):
                return nc.vector.tensor_scalar(dst, src, mv[:, t, 0:1], rstd[:, t:t + 1], ALU.subtract, ALU.mult)

            v.wait_ge(x_in, 16)
            first = root(mv[:, :, 1], LN_EPS, 1.0, 0, stats(lambda t: xin[:, t], 0, 0), 1)
            for t in range(NT):
                center(t, xin[:, t], xin[:, t]).then_inc(xln_ready, 1)

            with v.Fori(0, B) as b:
                base = v.snap(b * DVB + first)
                k = 0
                tpb = v.snap(b * TB)
                hib = tpb
                v.wait_ge(stored, b * 32 + 32)
                nc.vector.memset(racc[:], 0.0).then_inc(dve, 1)
                k += 1
                for t in range(NT):
                    v.wait_ge(tp_hi, hib + (t + 1))
                    c4 = xTl[:, :, t * P:(t + 1) * P]
                    nc.vector.tensor_tensor(c4, TP[:, t % 2].rearrange("p (c n) -> p c n", c=MC),
                                            xTh[:, :, t * P:(t + 1) * P].bitcast(F32), ALU.subtract).then_inc(tp_lo, 1)
                k0 = k
                with v.Fori(0, G) as g:
                    it = v.snap(b * G + g)
                    gb = v.snap(base + k0 + g * GD)
                    hi0 = v.snap(hib + NT + g * TG)

                    def lo_tile(t):
                        v.wait_ge(tp_hi, hi0 + (2 * t + 1))
                        nc.vector.tensor_tensor(qTl[:, :, t * P:(t + 1) * P], TP[:, 0].rearrange("p (h n) -> p h n", h=H),
                                                qTh[:, :, t * P:(t + 1) * P].bitcast(F32), ALU.subtract).then_inc(tp_lo, 1)
                        v.wait_ge(tp_hi, hi0 + (2 * t + 2))
                        nc.vector.tensor_tensor(kTl[:, t * P:(t + 1) * P], TP[:, 1, 0:P],
                                                kTh[:, t * P:(t + 1) * P].bitcast(F32), ALU.subtract).then_inc(tp_lo, 1)

                    def rope_start(t):
                        v.wait_ge(s_read, it * SG + t + 1 + 2)
                        tab = cos[:, t:t + 1, :].to_broadcast([P, 2 * (H + 1), HALF])
                        nc.vector.tensor_tensor(t1[t % 2].rearrange("p (h c) -> p h c", c=HALF),
                                                raw[t % 2][:, 0:RW].rearrange("p (h c) -> p h c", c=HALF),
                                                tab, ALU.mult).then_inc(dve, 1)
                        nc.vector.tensor_copy(vh[:, t], raw[t % 2][:, RW:PW]).then_inc(dve, 1)
                        v.wait_ge(dve, gb + (2 * t + 2))
                        nc.vector.tensor_tensor(vl[:, t], raw[t % 2][:, RW:PW], vh[:, t].bitcast(F32), ALU.subtract)

                    def rope_end(t):
                        v.wait_ge(crossed, it * NT + t + 1)
                        full, cross = (x[t % 2].rearrange("p (h s c) -> p h s c", s=2, c=HALF) for x in (t1, t2))
                        nc.vector.tensor_tensor(full[:, :, 0, :], full[:, :, 0, :], cross[:, :, 0, :], ALU.subtract)
                        nc.vector.tensor_tensor(full[:, :, 1, :], full[:, :, 1, :], cross[:, :, 1, :], ALU.add).then_inc(turned, 1)

                    for t in range(NT - 1):
                        if t >= 2:
                            lo_tile(t - 2)
                        rope_start(t)
                        rope_end(t)

                    def row_max(u, a):
                        ib = UNITS[u][0]
                        n = 2 * u + a
                        v.wait_ge(s_done, it * SG + NT + n + 1)
                        nc.vector.tensor_reduce(negmax[:, n % 4:n % 4 + 1], S[:, a, 0:(IB * ib + a + 1) * P], AX_X,
                                                ALU.max, negate=True).then_inc(max_ready, 1)

                    def recips(u):
                        for n in (2 * u, 2 * u + 1):
                            v.wait_ge(s_read, it * SG + NT + n + 1 + 2)
                            nc.vector.reciprocal(rinv[:, n % 4:n % 4 + 1], rsum[:, n % 4:n % 4 + 1]).then_inc(rinv_ready, 1)

                    def lo_pair(n):
                        u, jp = PAIRS[n]
                        w = 3 * P if jp == UNITS[u][0] else 4 * P
                        v.wait_ge(tp_hi, hi0 + (2 * NT + n + 1))
                        nc.vector.tensor_tensor(ptl[:, n % 2, 0:w], TP[:, n % 2, 0:w], pth[:, n % 2, 0:w].bitcast(F32),
                                                ALU.subtract).then_inc(tp_lo, 1)

                    def norm_out(u):
                        v.wait_ge(over_ready, it * len(UNITS) + u + 1)
                        nc.vector.tensor_tensor(onorm[:], bank("o", u)[:, 0:IB * P], onorm[:],
                                                ALU.mult).then_inc(o_free, 1)

                    def add_results(tiles):
                        for t in tiles:
                            v.wait_ge(r_done, it * NT + PROJECTED.index(t) + 1 + 1)
                            nc.vector.tensor_tensor(racc[:, t], racc[:, t], bank("r", t), ALU.add).then_inc(o_free, 1)
                            wait_apart(v, o_free, b * MB + g * MG + (OUTPUTS.index(("r", t)) + 1 + 2))
                            nc.vector.bn_stats(stat[:, t], racc[:, t]).then_inc(dve, 1)

                    lo_tile(NT - 3)
                    rope_start(NT - 1)
                    row_max(0, 0)
                    rope_end(NT - 1)
                    lo_tile(NT - 2)
                    row_max(0, 1)
                    row_max(1, 0)
                    lo_tile(NT - 1)
                    row_max(1, 1)
                    recips(0)
                    lo_pair(0)
                    for u, (ib, h) in enumerate(UNITS):
                        ahead = u + 2 < len(UNITS)
                        for jp in range(ib + 1):
                            n = PAIR_OF[(u, jp)] + 1
                            if n < NPAIR:
                                lo_pair(n)
                            if jp == ib and u + 1 < len(UNITS):
                                recips(u + 1)
                            if jp == 0:
                                add_results(PROJECT_AT.get(u, []))
                            if jp < 2 and ahead:
                                row_max(u + 2, jp)
                        if ib == 0 and ahead:
                            row_max(u + 2, 1)
                        norm_out(u)
                    add_results(PROJECT_LAST)
                k = k0
                base2 = v.snap(base + G * GD)
                v.wait_ge(x_in, b * 32 + 32)
                v.wait_ge(o_free, b * MB + (G * MG + 2))
                k = stats(None, base2, k, halves=True)
                k = root(mv[:, :, 1], LN_EPS, 1.0, base2, k, b * 4 + 2)
                for t in range(NT):
                    center(t, racc[:, t], racc[:, t]).then_inc(dve, 1)
                k += NT
                v.wait_ge(dve, base2 + k)
                nc.vector.tensor_tensor(racc[:], racc[:], xin, ALU.add).then_inc(out_ready, 1)
                v.wait_ge(out_ready, b * 2 + 1)
                k = stats(lambda t: racc[:, t], base2, k)
                k = root(mv[:, :, 1], LN_EPS, 1.0, base2, k, b * 4 + 3)
                for t in range(NT):
                    ins = center(t, racc[:, t], work[:, t])
                    ins.then_inc(out_ready if t == NT - 1 else sq_ready, 1)
                nc.vector.tensor_copy(coef[:, bass.ds(b * NT, NT), K], mv[:, :, 0])
                nc.vector.tensor_copy(coef[:, bass.ds(b * NT, NT), K + 1], rstd[:]).then_inc(dve, 1)
                k += 1
                v.wait_ge(sq_done, b * NT + NT)
                v.wait_ge(dve, base2 + k)
                k = root(ssq[:], RMS_EPS, 1.0 / M, base2, k, b * 4 + 4)
                for t in range(NT):
                    nc.vector.scalar_tensor_tensor(out=work[:, t], in0=work[:, t], scalar=rstd[:, t:t + 1], in1=nwb[:],
                                                   op0=ALU.mult, op1=ALU.mult).then_inc(h_ready, 1)
                for t in range(NT):
                    v.wait_ge(tp_hi, tpb + (NT + G * TG + t + 1))
                    nc.vector.tensor_tensor(ptl[:, t % 2], TP[:, t % 2], pth[:, t % 2].bitcast(F32), ALU.subtract).then_inc(tp_lo, 1)
                    if t == 0:
                        v.wait_ge(x_in, b * 32 + 48)
                    nc.vector.bn_stats(stat[:, t], xin[:, t]).then_inc(dve, 1)
                    k += 1
                    if t >= 1:
                        k = router(t - 1, b, base2, k)
                k = stats(None, base2, k, halves=True)
                k = root(mv[:, :, 1], LN_EPS, 1.0, base2, k, b * 4 + 5)
                for t in range(NT):
                    center(t, xin[:, t], xin[:, t]).then_inc(xln_ready, 1)
                k = router(NT - 1, b, base2, k)
                wait_apart(v, placed, b * NT + NT)
                nc.vector.tensor_copy(coef[:, bass.ds(b * NT, NT), 0:K], top8[:, :, 0:K])
                nc.vector.tensor_copy(topi[:, bass.ds(b * NT, NT), :], idx8[:, :, 0:K]).then_inc(dve, 1)
                k += 1
                assert k + G * GD == DVB, (k + G * GD, DVB)

        @block.scalar
        def _(act):
            act.sem_inc(s_read, 2)
            act.wait_ge(var_ready, 1)
            nc.scalar.activation(std[:], vareps[:], ACT.Sqrt).then_inc(std_ready, 1)
            with act.Fori(0, B) as b:
                for t in range(NT):
                    act.wait_ge(tp_done, b * TB + t + 1)
                    nc.scalar.copy(xTh[:, :, t * P:(t + 1) * P], TP[:, t % 2].rearrange("p (c n) -> p c n", c=MC)).then_inc(tp_hi, 1)
                with act.Fori(0, G) as g:
                    it = act.snap(b * G + g)
                    tp0 = act.snap(b * TB + NT + g * TG)

                    def hi_tile(t):
                        act.wait_ge(tp_done, tp0 + (2 * t + 1))
                        nc.scalar.copy(qTh[:, :, t * P:(t + 1) * P], TP[:, 0].rearrange("p (h n) -> p h n", h=H)).then_inc(tp_hi, 1)
                        act.wait_ge(tp_done, tp0 + (2 * t + 2))
                        nc.scalar.copy(kTh[:, t * P:(t + 1) * P], TP[:, 1, 0:P]).then_inc(tp_hi, 1)

                    for t in range(NT):
                        act.wait_ge(s_done, it * SG + t + 1)
                        if t >= 2:
                            act.wait_ge(turned, it * NT + t - 1)
                        nc.scalar.copy(raw[t % 2], S[:, t % 2, 0:PW]).then_inc(s_read, 1)
                        if 2 <= t < NT - 1:
                            hi_tile(t - 2)

                    def exp(u, a):
                        n = 2 * u + a
                        w = (IB * UNITS[u][0] + a + 1) * P
                        act.wait_ge(max_ready, it * 2 * len(UNITS) + n + 1)
                        nc.scalar.activation(probs(u, a)[:, 0:w], S[:, a, 0:w], ACT.Exp, bias=negmax[:, n % 4:n % 4 + 1],
                                             accum_out=rsum[:, n % 4:n % 4 + 1]).then_inc(s_read, 1)

                    def hi_pair(n):
                        u, jp = PAIRS[n]
                        w = 3 * P if jp == UNITS[u][0] else 4 * P
                        act.wait_ge(tp_done, tp0 + (2 * NT + n + 1))
                        act.wait_ge(pv_done, it * NPAIR + n + 1)
                        nc.scalar.copy(pth[:, n % 2, 0:w], TP[:, n % 2, 0:w]).then_inc(tp_hi, 1)

                    hi_tile(NT - 3)
                    exp(0, 0)
                    hi_tile(NT - 2)
                    exp(0, 1)
                    hi_tile(NT - 1)
                    exp(1, 0)
                    hi_pair(0)
                    exp(1, 1)
                    for u, (ib, h) in enumerate(UNITS):
                        ahead = u + 2 < len(UNITS)
                        late = 1 if u % 2 else 0
                        for jp in range(ib + 1):
                            n = PAIR_OF[(u, jp)] + 1
                            if n < NPAIR:
                                hi_pair(n)
                            if 0 <= jp - late < 2 and ahead:
                                exp(u + 2, jp - late)
                        act.wait_ge(pv_done, it * NPAIR + PAIR_OF[(u, ib)] + 1 + 2)
                        act.wait_ge(o_split, it * len(UNITS) + u + 1)
                        nc.scalar.copy(onorm[:], bank("o", u)[:, IB * P:2 * IB * P]).then_inc(over_ready, 1)
                        if ib == 0 and ahead:
                            exp(u + 2, 1)
                for r in (2, 3):
                    act.wait_ge(var_ready, b * 4 + r)
                    nc.scalar.activation(std[:], vareps[:], ACT.Sqrt).then_inc(std_ready, 1)
                for t in range(NT):
                    if t >= 4:
                        act.wait_ge(sq_done, b * NT + t - 3)
                    if t < NT - 1:
                        act.wait_ge(sq_ready, b * (NT - 1) + t + 1)
                    else:
                        act.wait_ge(out_ready, b * 2 + 2)
                    nc.scalar.activation(S[:, t // 2 % 2, t % 2 * M:(t % 2 + 1) * M], work[:, t], ACT.Square, accum_out=ssq[:, t:t + 1]).then_inc(sq_done, 1)
                act.wait_ge(var_ready, b * 4 + 4)
                nc.scalar.activation(std[:], vareps[:], ACT.Sqrt).then_inc(std_ready, 1)
                for t in range(NT):
                    act.wait_ge(tp_done, b * TB + (NT + G * TG + t + 1))
                    if t >= 2:
                        act.wait_ge(lg_done, b * NT + t - 1)
                    nc.scalar.copy(pth[:, t % 2], TP[:, t % 2]).then_inc(tp_hi, 1)
                act.wait_ge(var_ready, b * 4 + 5)
                nc.scalar.activation(std[:], vareps[:], ACT.Sqrt).then_inc(std_ready, 1)

        @block.tensor
        def _(pe):
            mm = nc.tensor.matmul

            def mm3(out, ah, al, bh, bl, first, last):
                mm(out, ah, bh, start=first, stop=False)
                mm(out, ah, bl, start=False, stop=False)
                return mm(out, al, bh, start=False, stop=last)

            pe.sem_inc(pv_done, 2)
            pe.sem_inc(r_done, 1)
            pe.wait_ge(const_in, 64)
            for c in range(MC):
                ins = nc.tensor.transpose(TP[:, 0, c * E:(c + 1) * E], rw[:, c * P:(c + 1) * P], cst[0:E, C_ID:C_ID + E])
            ins.then_inc(rwT_ps, 1)
            pe.wait_ge(rwT_sb, 2)
            pe.wait_ge(cast_ready, 1)
            with pe.Fori(0, B) as b:
                tpb = pe.snap(b * TB)
                mb = pe.snap(b * MB)
                for t in range(NT):
                    pe.wait_ge(xln_ready, b * NT + t + 1)
                    pe.wait_ge(tp_lo, tpb + (t + 1))
                    for c in range(MC):
                        ins = nc.tensor.transpose(TP[:, t % 2, c * P:(c + 1) * P], xin[:, t, c * P:(c + 1) * P], ident)
                    ins.then_inc(tp_done, 1)
                with pe.Fori(0, G) as g:
                    it = pe.snap(b * G + g)
                    tp0 = pe.snap(tpb + NT + g * TG)
                    m0 = pe.snap(mb + g * MG)

                    def project(t):
                        if t == 0:
                            pe.wait_ge(tp_lo, tpb + (NT + 2))
                            pe.wait_ge(stage_free, it * 10 + 6 + 2)
                        pe.wait_ge(s_read, it * SG + t + 1)
                        tok = slice(t * P, (t + 1) * P)
                        for c in range(MC):
                            first, last = c == 0, c == MC - 1
                            for cols in (slice(0, QW), slice(QW, PW)):
                                ins = mm3(S[:, t % 2, cols], xTh[:, c, tok], xTl[:, c, tok], wph[:, c, cols], wpl[:, c, cols], first, last)
                        ins.then_inc(s_done, 1)

                    def transpose_tile(t):
                        pe.wait_ge(turned, it * NT + t + 1)
                        pe.wait_ge(tp_lo, tp0 + (2 * t + 1))
                        for h in range(H):
                            ins = nc.tensor.transpose(TP[:, 0, h * P:(h + 1) * P], t1[t % 2][:, h * D:(h + 1) * D], ident)
                        ins.then_inc(tp_done, 1)
                        pe.wait_ge(tp_lo, tp0 + (2 * t + 2))
                        nc.tensor.transpose(TP[:, 1, 0:P], t1[t % 2][:, H * D:RW], ident).then_inc(tp_done, 1)

                    for t in range(NT):
                        project(t)
                        if 2 <= t < NT - 1:
                            transpose_tile(t - 2)

                    def scores(u, a):
                        ib, h = UNITS[u]
                        i = IB * ib + a
                        n = NT + 2 * u + a
                        w = (i + 1) * P
                        if u < 4:
                            last = i if u < 2 else NT - 1
                            pe.wait_ge(tp_lo, tp0 + (2 * (last + 1) + 2))
                        pe.wait_ge(s_read, it * SG + n + 1)
                        q = slice(i * P, (i + 1) * P)
                        for j0 in range(0, w, 512):
                            j1 = min(j0 + 512, w)
                            tail = j1 == w
                            ins = mm3(S[:, a, j0:j1], qTh[:, h, q], qTl[:, h, q], kTh[:, j0:j1], kTl[:, j0:j1], True, not tail)
                            if tail:
                                ins = mm(S[:, a, i * P:w], idb[:], mskb[:], start=False, stop=True)
                        ins.then_inc(s_done, 1)

                    def blocks(u, jp):
                        diag = jp == UNITS[u][0]
                        return [(jj, a) for jj in range(2) for a in range(IB) if not (diag and jj == 1 and a == 0)]

                    def transpose_pair(n):
                        u, jp = PAIRS[n]
                        if jp == 0:
                            pe.wait_ge(s_read, it * SG + NT + 2 * u + 2 + 2)
                        pe.wait_ge(tp_lo, tp0 + (2 * NT + n + 1))
                        for m, (jj, a) in enumerate(blocks(u, jp)):
                            j = 2 * jp + jj
                            ins = nc.tensor.transpose(TP[:, n % 2, m * P:(m + 1) * P], probs(u, a)[:, j * P:(j + 1) * P], ident)
                        ins.then_inc(tp_done, 1)

                    def spread(u):
                        pe.wait_ge(rinv_ready, it * 2 * len(UNITS) + 2 * u + 2)
                        for a in range(IB):
                            n = 2 * u + a
                            nc.tensor.transpose(bank("o", u)[:, (IB + a) * P:(IB + a + 1) * P],
                                                rinv[:, n % 4:n % 4 + 1].to_broadcast([P, P]), ident)

                    def value_pair(u, jp):
                        n = PAIR_OF[(u, jp)]
                        ib = UNITS[u][0]
                        pe.wait_ge(tp_lo, tp0 + (2 * NT + n + 1 + 2))
                        if jp == 0:
                            pe.wait_ge(o_free, m0 + (OUTPUTS.index(("o", u)) + 1))
                            spread(u)
                        m = 0
                        for jj in range(2):
                            a0 = 1 if (jp == ib and jj == 1) else 0
                            w = (IB - a0) * P
                            j = 2 * jp + jj
                            cols = slice(m * P, m * P + w)
                            ins = mm3(bank("o", u)[:, a0 * P:IB * P], vh[:, j], vl[:, j], pth[:, n % 2, cols], ptl[:, n % 2, cols],
                                      jp == 0 and jj == 0, jp == ib and jj == 1)
                            m += IB - a0
                        ins.then_inc(pv_done, 1)

                    def out_project(t):
                        ib, a = t // IB, t % IB
                        pe.wait_ge(o_free, m0 + (OUTPUTS.index(("r", t)) + 1))
                        if a == 0:
                            last = max(u for u in range(len(UNITS)) if UNITS[u][0] == ib)
                            pe.wait_ge(o_split, it * len(UNITS) + last + 1 + 1)
                            pe.wait_ge(stage_free, it * 10 + 10 + 2)
                        for h in range(H):
                            place = ib // (NIB // 2), h, slice(a * P, (a + 1) * P)
                            ins = mm3(bank("r", t), oTh[:, *place], oTl[:, *place], woh[:, h], wol[:, h], h == 0, h == H - 1)
                        ins.then_inc(r_done, 1)

                    transpose_tile(NT - 3)
                    scores(0, 0)
                    transpose_tile(NT - 2)
                    scores(0, 1)
                    scores(1, 0)
                    transpose_tile(NT - 1)
                    scores(1, 1)
                    transpose_pair(0)
                    for u, (ib, h) in enumerate(UNITS):
                        ahead = u + 2 < len(UNITS)
                        for jp in range(ib + 1):
                            n = PAIR_OF[(u, jp)] + 1
                            if n < NPAIR:
                                transpose_pair(n)
                            for t in PROJECT_AT.get(u, []) if jp == 0 else []:
                                out_project(t)
                            if jp < 2 and ahead:
                                scores(u + 2, jp)
                            value_pair(u, jp)
                        if ib == 0 and ahead:
                            scores(u + 2, 1)
                    for t in PROJECT_LAST:
                        out_project(t)

                def route(t):
                    n = G * MG + t
                    pe.wait_ge(o_free, mb + (n + 1))
                    pe.wait_ge(tp_lo, tpb + (NT + G * TG + t + 1 + 2))
                    for c in range(MC):
                        cols = slice(c * P, (c + 1) * P)
                        ins = mm3(O[:, n % 2, 0:E], pth[:, t % 2, cols], ptl[:, t % 2, cols], rwTh[:, c], rwTl[:, c], c == 0, c == MC - 1)
                    ins.then_inc(lg_done, 1)

                for t in range(NT):
                    n = NT + G * TG + t
                    pe.wait_ge(h_ready, b * NT + t + 1)
                    pe.wait_ge(tp_lo, tpb + (n + 1))
                    for c in range(MC):
                        ins = nc.tensor.transpose(TP[:, t % 2, c * P:(c + 1) * P], work[:, t, c * P:(c + 1) * P], ident)
                    ins.then_inc(tp_done, 1)
                    if t >= 1:
                        route(t - 1)
                route(NT - 1)


def dispatch(nc, sg, su, sd, w1, w2, const, topi, slots, coef, ids, etab, ctab, wh, wl, raww):
    with ExitStack() as ctx:
        def sb(name, shape, dt=F32):
            return ctx.enter_context(nc.sbuf_tensor(name, shape, dt))

        def sem(name):
            return ctx.enter_context(nc.semaphore(name))

        cst = sb("cst2", [P, C_W])
        stage = sb("stage2", [P, 2, M])
        gate = sb("gate", [P, NTILE, K])
        trib, oneb = sb("trib", [P, P], BF16), sb("oneb", [P, P], BF16)
        hot = sb("hot", [P, K, NTILE, E])
        anyb = sb("anyb", [P, NTILE, E], BF16)
        tot, cumA, cumB, place = (sb(n, [P, NTILE, E]) for n in ("tot", "cumA", "cumB", "place"))
        idxf, slotf = sb("idxf", [P, NTILE, K]), sb("slotf", [P, NTILE, K])
        sloti, tmpi = sb("sloti", [P, NTILE, K], I32), sb("tmpi", [P, NTILE, K], I32)
        tilef, posf = sb("tilef", [P, NTILE, K]), sb("posf", [P, NTILE, K])
        nti, ntf, ca, cb = sb("nti", [P, E], I32), sb("ntf", [P, E]), sb("ca", [P, E]), sb("cb", [P, E])
        par = sb("par", [P, 2], I32)
        base = sb("basef", [P, E])
        over = sb("over", [P, XW, E])
        etf = sb("etf", [P, XW])
        selp, selt = sb("selp", [P, 2, K, P], F32R), sb("selt", [P, 2, K, XW], F32R)
        zero = sb("zero2", [P, XW], F32R)
        gs, gr = sb("gs", [P, NTILE]), sb("gr", [P, NTILE])

        S = ctx.enter_context(nc.psum_tensor("S2", [P, 2, 512], F32))
        I = ctx.enter_context(nc.psum_tensor("I2", [P, 512], F32))
        C = ctx.enter_context(nc.psum_tensor("C2", [P, 2, 512], F32))

        const_in = sem("const_in2")
        staged, stage_free, w_hi = [sem("staged20"), sem("staged21")], sem("stage_free2"), sem("w_hi2")
        experts_in = sem("experts_in")
        step = sem("step")
        any_ready, counted = sem("any_ready"), sem("counted")
        sel_ready, listed = sem("sel_ready"), sem("listed")
        gd_ready, ge_ready = sem("gd_ready"), sem("ge_ready")

        block = ctx.enter_context(nc.Block())

        @block.sync
        def _(sp):
            sp.dma_start(cst[:], const).then_inc(const_in, 16)
            for n in range(3 * MC):
                if n >= 2:
                    sp.wait_ge(stage_free, n - 1)
                w = (sg, su, sd)[n // MC].rearrange("(c p) f -> c p f", p=P)[n % MC]
                sp.dma_start(stage[:, n % 2], w).then_inc(staged[n % 2], 16)
            for e in range(2):
                load_expert(sp, raww, e, w1[e], w2[e], experts_in)
            sp.wait_ge(experts_in, 64)

        @block.gpsimd
        def _(pool):
            for n in range(3 * MC):
                hi, lo = wh[:, n // MC, n % MC], wl[:, n // MC, n % MC]
                pool.wait_ge(staged[n % 2], 16 * (n // 2 + 1))
                nc.gpsimd.tensor_scalar(hi, stage[:, n % 2], 1.0, 1.0, ALU.mult, ALU.mult).then_inc(w_hi, 1)
                pool.wait_ge(w_hi, n + 1)
                nc.gpsimd.tensor_tensor(lo, stage[:, n % 2], hi.bitcast(F32), ALU.subtract).then_inc(stage_free, 1)

        @block.vector
        def _(v):
            done = [0]

            def link(ins):
                done[0] += 1
                ins.then_inc(step, 1)
                v.wait_ge(step, done[0])

            def prefix(src, bufs, n, cut):
                for r in range((n - 1).bit_length()):
                    d, dst = 1 << r, bufs[r % 2]
                    nc.vector.tensor_copy(cut(dst, 0, d), cut(src, 0, d))
                    link(nc.vector.tensor_tensor(cut(dst, d, n), cut(src, d, n), cut(src, 0, n - d), ALU.add))
                    src = dst
                return src

            v.wait_ge(const_in, 16)
            nc.vector.tensor_copy(trib[:], cst[:, C_TRI:C_TRI + P])
            nc.vector.memset(zero[:].bitcast(F32), 0.0)
            nc.vector.memset(oneb[:], 1.0)
            nc.vector.tensor_tensor(gate[:], coef[:, :, 0:K], coef[:, :, 0:1].to_broadcast([P, NTILE, K]), ALU.subtract).then_inc(gd_ready, 1)
            link(nc.vector.tensor_copy(idxf[:], topi[:, :, 0:K]))
            iota_e = cst[:, C_IOTA:C_IOTA + E].rearrange("p (o e) -> p o e", o=1).to_broadcast([P, NTILE, E])
            for k in range(K):
                ins = nc.vector.tensor_tensor(hot[:, k], iota_e, idxf[:, :, k:k + 1].to_broadcast([P, NTILE, E]), ALU.is_equal)
            link(ins)
            nc.vector.tensor_tensor(cumA[:], hot[:, 0], hot[:, 1], ALU.add)
            link(nc.vector.tensor_tensor(cumB[:], hot[:, 2], hot[:, 3], ALU.add))
            nc.vector.tensor_tensor(anyb[:], cumA[:], cumB[:], ALU.add).then_inc(any_ready, 1)
            v.wait_ge(counted, 1)
            link(nc.vector.tensor_copy(tot[:], S[:].rearrange("p a (t e) -> p (a t) e", e=E)))
            cum = prefix(tot, (cumA, cumB), NTILE, lambda x, a, b: x[:, a:b])
            link(nc.vector.tensor_tensor(place[:], cum[:], tot[:], ALU.subtract))
            link(nc.vector.tensor_tensor(place[:], place[:], C[:].rearrange("p a (t e) -> p (a t) e", e=E), ALU.add))
            link(nc.vector.tensor_scalar(nti[:], cum[:, NTILE - 1], P - 1.0, None, ALU.add))
            link(nc.vector.tensor_scalar(nti[:], nti[:], 7, None, ALU.arith_shift_right))
            link(nc.vector.tensor_scalar(ntf[:], nti[:], 1.0, None, ALU.max))
            ends = prefix(ntf, (ca, cb), E, lambda x, a, b: x[:, a:b])
            link(nc.vector.tensor_tensor(base[:], ends[:], ntf[:], ALU.subtract))
            link(nc.vector.tensor_scalar(base[:], base[:], float(P), None, ALU.mult))
            link(nc.vector.tensor_copy(par[:, 0:1], ends[:, E - 1:E]))
            link(nc.vector.tensor_scalar(par[:, 1:2], par[:, 0:1], 1, None, ALU.bitwise_and))
            link(nc.vector.tensor_tensor(ends[:, E - 1:E], ends[:, E - 1:E], par[:, 1:2], ALU.add))
            nc.vector.memset(ctab[:], 0)
            iota_t = cst[:, C_IOTA:C_IOTA + XW].rearrange("p (t o) -> p t o", o=1).to_broadcast([P, XW, E])
            link(nc.vector.tensor_tensor(over[:], iota_t, ends[:].rearrange("p (o e) -> p o e", o=1).to_broadcast([P, XW, E]), ALU.is_ge))
            nc.vector.tensor_copy(ctab[:, 1:E + 1], ends[:])
            link(nc.vector.tensor_reduce(etf[:], over[:], AX_X, ALU.add))
            nc.vector.memset(etab[:], 0)
            link(nc.vector.tensor_scalar(etf[:], etf[:], E - 1.0, None, ALU.min))
            nc.vector.tensor_copy(etab[:, 1:XW + 1], etf[:])
            link(nc.vector.tensor_tensor(place[:], place[:], base[:].rearrange("p (o e) -> p o e", o=1).to_broadcast([P, NTILE, E]), ALU.add))
            for k in range(K):
                ins = nc.vector.tensor_tensor(hot[:, k], hot[:, k], place[:], ALU.mult)
            link(ins)
            for k in range(K):
                ins = nc.vector.tensor_reduce(slotf[:, :, k], hot[:, k], AX_X, ALU.add)
            link(ins)
            link(nc.vector.tensor_copy(sloti[:], slotf[:]))
            nc.vector.tensor_scalar(slots[:], slotf[:], float(P), None, ALU.add)
            link(nc.vector.tensor_scalar(tmpi[:], sloti[:], 7, None, ALU.arith_shift_right))
            link(nc.vector.tensor_copy(tilef[:], tmpi[:]))
            link(nc.vector.tensor_scalar(tmpi[:], sloti[:], P - 1, None, ALU.bitwise_and))
            link(nc.vector.tensor_copy(posf[:], tmpi[:]))
            v.wait_ge(ge_ready, 1)
            link(nc.vector.tensor_reduce(gs[:], gate[:], AX_X, ALU.add))
            link(nc.vector.reciprocal(gr[:], gs[:]))
            nc.vector.tensor_tensor(coef[:, :, 0:K], gate[:], gr[:].rearrange("p (t o) -> p t o", o=1).to_broadcast([P, NTILE, K]), ALU.mult)
            v.sem_inc(sel_ready, 1)
            v.sem_inc(listed, 1)
            with v.Fori(0, NTILE // 2) as j:
                for s in range(2):
                    i = v.snap(j * 2 + s)
                    wait_apart(v, listed, i + 1)
                    for k in range(K):
                        nc.vector.tensor_scalar(selp[:, s, k], cst[:, C_IOTA:C_IOTA + P], posf[:, bass.ds(i, 1), k], None, ALU.is_equal)
                        ins = nc.vector.tensor_scalar(selt[:, s, k], cst[:, C_IOTA:C_IOTA + XW], tilef[:, bass.ds(i, 1), k],
                                                      cst[:, bass.ds(i + C_TOK, 1)], ALU.is_equal, ALU.mult)
                    ins.then_inc(sel_ready, 1)
            v.wait_ge(listed, NTILE + 3)
            nc.vector.tensor_copy(ids[:], I[:, 0:XW])

        @block.scalar
        def _(act):
            act.wait_ge(gd_ready, 1)
            nc.scalar.activation(gate[:], gate[:], ACT.Exp).then_inc(ge_ready, 1)

        @block.tensor
        def _(pe):
            mm = nc.tensor.matmul

            pe.wait_ge(const_in, 16)
            pe.wait_ge(any_ready, 1)
            flat = anyb[:].rearrange("p t e -> p (t e)")
            for a in range(2):
                mm(C[:, a], trib[:], flat[:, a * 512:(a + 1) * 512], start=True, stop=True)
                ins = mm(S[:, a], oneb[:], flat[:, a * 512:(a + 1) * 512], start=True, stop=True)
            ins.then_inc(counted, 1)
            pe.wait_ge(sel_ready, 1)
            mm(I[:, 0:XW], zero[:, 0:P], zero[:], start=True, stop=False).then_inc(listed, 1)
            with pe.Fori(0, NTILE // 2) as j:
                for s in range(2):
                    pe.wait_ge(sel_ready, j * 2 + (s + 2))
                    for k in range(K):
                        ins = mm(I[:, 0:XW], selp[:, s, k], selt[:, s, k], start=False, stop=False)
                    ins.then_inc(listed, 1)
            mm(I[:, 0:XW], zero[:, 0:P], zero[:], start=False, stop=True).then_inc(listed, 1)


def experts(nc, w1, w2, const, h_d, y_d, ids, etab, ctab, raww):
    with ExitStack() as ctx:
        def sb(name, shape, dt=F32):
            return ctx.enter_context(nc.sbuf_tensor(name, shape, dt))

        def sem(name):
            return ctx.enter_context(nc.semaphore(name))

        QC = WC // 3
        idn = sb("idn", [P, P])
        wh, wl = sb("weh", [P, 2, WC], F32R), sb("wel", [P, 2, WC], F32R)
        idx = sb("idx3", [P, 2], I32)
        xg = sb("xg", [P, 2, M])
        hTh, hTl = sb("hTh3", [P, MC, P], F32R), sb("hTl3", [P, MC, P], F32R)
        aTh, aTl = sb("aTh3", [P, FI], F32R), sb("aTl3", [P, FI], F32R)
        sl, ac = sb("sl3", [P, FI]), sb("ac3", [P, FI])
        yb = sb("yb", [P, 2, M])
        blank = sb("blank", [P, M])

        S = ctx.enter_context(nc.psum_tensor("S3", [P, 512], F32))
        TP = ctx.enter_context(nc.psum_tensor("TP3", [P, 2, 512], F32))
        O = ctx.enter_context(nc.psum_tensor("O3", [P, 512], F32))

        const_in = sem("const_in3")
        raw_in = [sem("raw_in0"), sem("raw_in1")]
        wh_ready, wl_ready = sem("wh_ready"), sem("wl_ready")
        idx_ready = sem("idx_ready")
        x_in = [sem("xg_in0"), sem("xg_in1")]
        t_done, hh_done, hl_done = sem("t_done3"), sem("hh_done3"), sem("hl_done3")
        gu_done, silu_done, act_ready = sem("gu_done3"), sem("silu_done3"), sem("act_ready3")
        at_done, ah_done, al_done = sem("at_done3"), sem("ah_done3"), sem("al_done3")
        dn_done, y_ready = sem("dn_done3"), sem("y_ready3")
        y_out = [sem("y_out0"), sem("y_out1")]

        block = ctx.enter_context(nc.Block())

        blank_ready, blank_out = sem("blank_ready"), sem("blank_out")
        y_stored, y_free = sem("y_stored"), sem("y_free")

        def total(eng):
            return eng.value_load(ctab[0:1, E:E + 1], min_val=4, max_val=XT)

        @block.sync
        def _(sp):
            sp.dma_start(idn[:], const[:, C_ID:C_ID + P]).then_inc(const_in, 16)
            sp.sem_inc(y_free, 2)
            y_t = y_d.rearrange("(t p) m -> t p m", p=P)

            def store(n, s):
                sp.wait_ge(y_ready, n + 1)
                sp.dma_start(y_t[n], yb[:, s]).then_inc(y_stored, 16)
                sp.wait_ge(y_stored, n * 16 + 16)
                sp.sem_inc(y_free, 1)

            store(0, 0)
            pairs = sp.snap(total(sp) // 2)
            with sp.Fori(0, pairs) as j:
                store(sp.snap(j * 2 + 1), 1)
                store(sp.snap(j * 2 + 2), 0)

        @block.gpsimd
        def _(pool):
            h_rows = h_d.rearrange("b t m -> (b t) m")

            def gather(t, s):
                wait_apart(pool, t_done, t + 1)
                nc.gpsimd.tensor_copy(idx[:, s:s + 1], ids[:, bass.ds(t, 1)]).then_inc(idx_ready, 1)
                wait_apart(pool, idx_ready, t + 1)
                nc.gpsimd.indirect_dma_start(xg[:, s], None, h_rows, bass.IndirectOffsetOnAxis(ap=idx[:, s:s + 1], axis=0)).then_inc(x_in[s], 16)

            gather(0, 0)
            tiles = pool.snap(total(pool))
            y_t = y_d.rearrange("(t p) m -> t p m", p=P)
            pool.wait_ge(blank_ready, 1)
            with pool.Fori(0, XT - tiles) as r:
                pool.dma_start(y_t[nc.s_assert_within(XT - r, 1, XT)], blank[:]).then_inc(blank_out, 16)
            pairs = pool.snap(tiles // 2)
            with pool.Fori(0, pairs) as j:
                gather(pool.snap(j * 2 + 1), 1)
                gather(pool.snap(j * 2 + 2), 0)
            with pool.Fori(0, XT - tiles) as r:
                pool.wait_ge(blank_out, r * 16 + 16)

        def third(r):
            return bass.ds(nc.s_assert_within(r * QC, 0, 2 * QC, skip_runtime_bounds_check_because="it stands under If r < 3"), QC)

        @block.scalar
        def _(act):
            def load(e, s):
                load_expert(act, raww, s, w1[e], w2[e], raw_in[s])

            def hi_h(t):
                act.wait_ge(t_done, t + 1 + 2)
                nc.scalar.copy(flatten(hTh), TP[:, 0]).then_inc(hh_done, 1)

            def result(n):
                wait_apart(act, dn_done, n + 1)
                act.wait_ge(y_free, n + 1)
                nc.scalar.copy(yb[:, n % 2, :], O[:]).then_inc(y_ready, 1)

            for s in range(2):
                act.sem_inc(raw_in[s], 32)
            for r in range(3):
                nc.scalar.copy(wh[:, 0, r * QC:(r + 1) * QC], raww[:, 0, r * QC:(r + 1) * QC]).then_inc(wh_ready, 1)
            hi_h(0)
            with act.Fori(0, E // 2) as j:
                for s in range(2):
                    e = act.snap(j * 2 + s)
                    act.wait_ge(wl_ready, e * 3 + 3)
                    load((e + 2) % E, s)
                    t0 = act.value_load(ctab[0:1, bass.ds(e, 1)], min_val=0, max_val=XT)
                    t1 = act.value_load(ctab[0:1, bass.ds(e + 1, 1)], min_val=1, max_val=XT)
                    wait_apart(act, raw_in[1 - s], j * 32 + 32 * (s + 1))
                    with act.Fori(0, t1 - t0) as r:
                        t = act.snap(t0 + r)
                        act.wait_ge(gu_done, t + 1)
                        nc.scalar.activation(sl[:], S[:, 0:FI], ACT.Silu).then_inc(silu_done, 1)
                        hi_h(t + 1)
                        result(t)
                        act.wait_ge(at_done, t + 1)
                        nc.scalar.copy(aTh[:], TP[:, 1, 0:FI]).then_inc(ah_done, 1)
                        with act.If(r < 3):
                            nc.scalar.copy(wh[:, 1 - s, third(r)], raww[:, 1 - s, third(r)]).then_inc(wh_ready, 1)
                    for m in (1, 2):
                        with act.If(t1 < t0 + (m + 1)):
                            wait_apart(act, dn_done, t0 + 1)
                            nc.scalar.copy(wh[:, 1 - s, m * QC:(m + 1) * QC], raww[:, 1 - s, m * QC:(m + 1) * QC]).then_inc(wh_ready, 1)
            result(total(act))
            for s in range(2):
                act.wait_ge(raw_in[s], 32 * (E // 2 + 1))

        @block.vector
        def _(v):
            nc.vector.memset(blank[:], 0.0).then_inc(blank_ready, 1)
            nc.vector.memset(aTh[:].bitcast(F32), 0.0)
            nc.vector.memset(aTl[:].bitcast(F32), 0.0).then_inc(al_done, 1)

            def split_lo(s, at, count):
                wait_apart(v, wh_ready, count)
                nc.vector.tensor_tensor(wl[:, s, at], raww[:, s, at], wh[:, s, at].bitcast(F32), ALU.subtract).then_inc(wl_ready, 1)

            def lo_h(t):
                v.wait_ge(hh_done, t + 1)
                nc.vector.tensor_tensor(flatten(hTl), TP[:, 0], flatten(hTh).bitcast(F32), ALU.subtract).then_inc(hl_done, 1)

            for r in range(3):
                split_lo(0, slice(r * QC, (r + 1) * QC), r + 1)
            lo_h(0)
            with v.Fori(0, E // 2) as j:
                for s in range(2):
                    e = v.snap(j * 2 + s)
                    t0 = v.value_load(ctab[0:1, bass.ds(e, 1)], min_val=0, max_val=XT)
                    t1 = v.value_load(ctab[0:1, bass.ds(e + 1, 1)], min_val=1, max_val=XT)
                    with v.Fori(0, t1 - t0) as r:
                        t = v.snap(t0 + r)
                        v.wait_ge(silu_done, t + 1)
                        nc.vector.tensor_tensor(ac[:], sl[:], S[:, FI:2 * FI], ALU.mult).then_inc(act_ready, 1)
                        lo_h(t + 1)
                        v.wait_ge(ah_done, t + 1)
                        nc.vector.tensor_tensor(aTl[:], TP[:, 1, 0:FI], aTh[:].bitcast(F32), ALU.subtract).then_inc(al_done, 1)
                        with v.If(r < 3):
                            split_lo(1 - s, third(r), e * 3 + 3 + r + 1)
                    for m in (1, 2):
                        with v.If(t1 < t0 + (m + 1)):
                            split_lo(1 - s, slice(m * QC, (m + 1) * QC), e * 3 + 3 + m + 1)

        @block.tensor
        def _(pe):
            mm = nc.tensor.matmul
            whf, wlf = (w[:].rearrange("p s c -> p (s c)") for w in (wh, wl))

            def mm3(out, ah, al, bh, bl, first, last):
                mm(out, ah, bh, start=first, stop=False)
                mm(out, ah, bl, start=False, stop=False)
                return mm(out, al, bh, start=False, stop=last)

            def expert_of(t):
                return pe.value_load(etab[0:1, bass.ds(t + 1, 1)], min_val=0, max_val=E - 1)

            def transpose_x(t, q, s):
                pe.wait_ge(x_in[s], q * 16 + 16)
                for c in range(MC):
                    ins = nc.tensor.transpose(TP[:, 0, c * P:(c + 1) * P], xg[:, s, c * P:(c + 1) * P], idn[:])
                ins.then_inc(t_done, 1)

            def down(t, place):
                pe.wait_ge(al_done, t + 2)
                for c in range(FI // P):
                    at = bass.ds(place * WC + (MC + c) * M, M)
                    ins = mm3(O[:], aTh[:, c * P:(c + 1) * P], aTl[:, c * P:(c + 1) * P], whf[:, at], wlf[:, at], c == 0, c == FI // P - 1)
                ins.then_inc(dn_done, 1)

            def gate_up(t, place, parts):
                pe.wait_ge(wl_ready, parts)
                pe.wait_ge(hl_done, t + 1)
                for c in range(MC):
                    at = bass.ds(place + c * M, M)
                    ins = mm3(S[:], hTh[:, c], hTl[:, c], whf[:, at], wlf[:, at], c == 0, c == MC - 1)
                ins.then_inc(gu_done, 1)

            def tile(t, q, s, first=False):
                transpose_x(t + 1, q + s, 1 - s)
                if not first:
                    before = pe.snap(expert_of(t - 1) % 2)
                    pe.wait_ge(y_ready, t)
                    down(t - 1, before)
                behind = expert_of(t + 1)
                place = pe.snap(pe.to_reg((behind % 2) * WC), min_val=0, max_val=WC)
                parts = pe.snap(pe.to_reg(behind * 3 + 3), min_val=3, max_val=3 * E)
                pe.wait_ge(act_ready, t + 1)
                for c in range(FI // P):
                    ins = nc.tensor.transpose(TP[:, 1, c * P:(c + 1) * P], ac[:, c * P:(c + 1) * P], idn[:])
                ins.then_inc(at_done, 1)
                return place, parts

            pe.sem_inc(t_done, 2)
            pe.wait_ge(const_in, 16)
            transpose_x(0, 0, 0)
            pe.wait_ge(wl_ready, 3)
            down(-1, 0)
            gate_up(0, 0, 3)
            gate_up(1, *tile(0, 0, 0, first=True))
            gate_up(2, *tile(1, 0, 1))
            pairs = pe.snap(total(pe) // 2)
            with pe.Fori(1, pairs) as j:
                for s in range(2):
                    t = pe.snap(j * 2 + s)
                    gate_up(t + 1, *tile(t, j, s))
            n = pe.snap(pairs * 2)
            before = pe.snap(expert_of(n - 1) % 2)
            pe.wait_ge(y_ready, n)
            down(n - 1, before)


def finish(nc, const, h_d, x2_d, y_d, out, slots, coef, wh, wl):
    with ExitStack() as ctx:
        def sb(name, shape, dt=F32):
            return ctx.enter_context(nc.sbuf_tensor(name, shape, dt))

        def sem(name):
            return ctx.enter_context(nc.semaphore(name))

        idn = sb("idn4", [P, P])
        hb = sb("hb", [P, 2, M])
        hTh, hTl = sb("hTh4", [P, MC, P], F32R), sb("hTl4", [P, MC, P], F32R)
        aTh, aTl = sb("aTh4", [P, MC, P], F32R), sb("aTl4", [P, MC, P], F32R)
        sl, ac = sb("sl4", [P, FS]), sb("ac4", [P, FS])
        idx = sb("idx4", [P, 2, K], I32)
        yg = sb("yg", [P, 2, K, M])
        acc, x2, ob = sb("acc4", [P, 2, M]), sb("x24", [P, 2, M]), sb("ob4", [P, 2, M])
        ct = sb("ct4", [P, 2, K + 2])
        stat, mv = sb("stat4", [P, 2, 6]), sb("mv4", [P, 2, 2])
        ve, std, rstd = sb("ve4", [P, 2]), sb("std4", [P, 2]), sb("rstd4", [P, 2])

        S = ctx.enter_context(nc.psum_tensor("S4", [P, 2, 512], F32))
        TP = ctx.enter_context(nc.psum_tensor("TP4", [P, 2, 512], F32))
        O = ctx.enter_context(nc.psum_tensor("O4", [P, 512], F32))

        const_in = sem("const_in4")
        h_in, x_in = [sem("h_in0"), sem("h_in1")], [sem("x2_in0"), sem("x2_in1")]
        y_in = [sem("y_in0"), sem("y_in1")]
        idx_ready = sem("idx_ready4")
        step, end_step = sem("step4"), sem("end_step4")
        var_ready, std_ready = sem("var_ready4"), sem("std_ready4")
        t_done, hh_done, hl_done = sem("t_done4"), sem("hh_done4"), sem("hl_done4")
        gu_done, silu_done, act_ready = sem("gu_done4"), sem("silu_done4"), sem("act_ready4")
        at_done, ah_done, al_done = sem("at_done4"), sem("ah_done4"), sem("al_done4")
        dn_done, o_read = sem("dn_done4"), sem("o_read4")
        out_ready = sem("out_ready4")
        out_stored = [sem("out_stored0"), sem("out_stored1")]

        block = ctx.enter_context(nc.Block())
        HALVES = NTILE // 2
        WEIGH, END = 2 + K, 4

        @block.sync
        def _(sp):
            h_t = h_d.rearrange("b (t p) m -> (b t) p m", p=P)
            x2_t = x2_d.rearrange("b (t p) m -> (b t) p m", p=P)
            out_t = out.rearrange("b (t p) m -> (b t) p m", p=P)
            sp.dma_start(idn[:], const[:, C_ID:C_ID + P]).then_inc(const_in, 16)
            for s in range(2):
                sp.sem_inc(out_stored[s], 16)
                sp.dma_start(hb[:, s], h_t[s]).then_inc(h_in[s], 16)
                sp.dma_start(x2[:, s], x2_t[s]).then_inc(x_in[s], 16)
            with sp.Fori(0, HALVES) as j:
                for s in range(2):
                    i = sp.snap(j * 2 + s)
                    nxt = sp.snap((i + 2) % NTILE)
                    sp.wait_ge(out_ready, i + 1)
                    sp.dma_start(out_t[i], ob[:, s]).then_inc(out_stored[s], 16)
                    sp.dma_start(x2[:, s], x2_t[nxt]).then_inc(x_in[s], 16)
            for s in range(2):
                sp.wait_ge(out_stored[s], 16 * (HALVES + 1))
                sp.wait_ge(x_in[s], 16 * (HALVES + 1))

        @block.gpsimd
        def _(pool):
            with pool.Fori(0, HALVES) as j:
                for s in range(2):
                    i = pool.snap(j * 2 + s)
                    wait_apart(pool, step, i * WEIGH + WEIGH)
                    nc.gpsimd.tensor_copy(idx[:, s, :], slots[:, bass.ds(i, 1), :]).then_inc(idx_ready, 1)
                    wait_apart(pool, idx_ready, i + 1)
                    for k in range(K):
                        nc.gpsimd.indirect_dma_start(yg[:, s, k], None, y_d,
                                                     bass.IndirectOffsetOnAxis(ap=idx[:, s, k:k + 1], axis=0)).then_inc(y_in[s], 16)

        @block.vector
        def _(v):
            v.sem_inc(step, 2 * WEIGH)
            v.sem_inc(end_step, END)

            def lo_h(i):
                v.wait_ge(hh_done, i + 1)
                nc.vector.tensor_tensor(flatten(hTl), TP[:, 0], flatten(hTh).bitcast(F32), ALU.subtract).then_inc(hl_done, 1)

            def residual(i, q, s, c):
                wait_apart(v, x_in[s], q * 16 + 16)
                nc.vector.tensor_copy(ct[:, s, :], coef[:, bass.ds(i, 1), :]).then_inc(step, 1)
                wait_apart(v, step, c + 1)
                nc.vector.tensor_scalar(acc[:, s], x2[:, s], ct[:, s, K:K + 1], ct[:, s, K + 1:K + 2],
                                        ALU.subtract, ALU.mult).then_inc(step, 1)
                v.wait_ge(y_in[s], q * 64 + 64)

            def weigh(k, s, c):
                wait_apart(v, step, c + 2 + k)
                nc.vector.scalar_tensor_tensor(out=acc[:, s], in0=yg[:, s, k], scalar=ct[:, s, k:k + 1], in1=acc[:, s],
                                               op0=ALU.mult, op1=ALU.add).then_inc(step, 1)

            def add_shared(i, s, c):
                wait_apart(v, step, c)
                v.wait_ge(dn_done, i + 1)
                nc.vector.tensor_tensor(acc[:, s], acc[:, s], O[:], ALU.add).then_inc(o_read, 1)

            def tile(i, q, s, first=False, last=False):
                o = 1 - s
                c, e = v.snap(i * WEIGH + 2 * WEIGH), v.snap(i * END)
                if not last:
                    v.wait_ge(silu_done, i + 1)
                    nc.vector.tensor_tensor(ac[:], sl[:], S[:, 1], ALU.mult).then_inc(act_ready, 1)
                    lo_h(i + 1)
                    residual(i, q, s, c)
                    weigh(0, s, c)
                if not first:
                    add_shared(i - 1, o, c)
                if not last:
                    weigh(1, s, c)
                if not first:
                    wait_apart(v, o_read, i)
                    nc.vector.bn_stats(stat[:, o], acc[:, o]).then_inc(end_step, 1)
                if not last:
                    v.wait_ge(ah_done, i + 1)
                    nc.vector.tensor_tensor(flatten(aTl), TP[:, 1], flatten(aTh).bitcast(F32), ALU.subtract).then_inc(al_done, 1)
                if not first:
                    wait_apart(v, end_step, e + 1)
                    nc.vector.bn_aggr(mv[:, o], stat[:, o]).then_inc(end_step, 1)
                if not last:
                    weigh(2, s, c)
                if not first:
                    wait_apart(v, end_step, e + 2)
                    nc.vector.tensor_scalar(ve[:, o:o + 1], mv[:, o, 1:2], LN_EPS, None, ALU.add).then_inc(var_ready, 1)
                if not last:
                    weigh(3, s, c)
                if not first:
                    v.wait_ge(std_ready, i)
                    nc.vector.reciprocal(rstd[:, o:o + 1], std[:, o:o + 1]).then_inc(end_step, 1)
                    wait_apart(v, end_step, e + 3)
                    v.wait_ge(out_stored[o], (q if s else q - 1) * 16 + 16)
                    nc.vector.tensor_scalar(ob[:, o], acc[:, o], mv[:, o, 0:1], rstd[:, o:o + 1],
                                            ALU.subtract, ALU.mult).then_inc(end_step, 1)
                    wait_apart(v, end_step, e + 4)
                    nc.vector.tensor_tensor(ob[:, o], ob[:, o], x2[:, o], ALU.add).then_inc(out_ready, 1)

            lo_h(0)
            tile(0, 0, 0, first=True)
            tile(1, 0, 1)
            with v.Fori(1, HALVES) as j:
                for s in range(2):
                    tile(v.snap(j * 2 + s), j, s)
            tile(NTILE, HALVES, 0, last=True)

        @block.scalar
        def _(act):
            h_t = h_d.rearrange("b (t p) m -> (b t) p m", p=P)

            def hi_h(i, s):
                act.wait_ge(t_done, i + 1)
                nc.scalar.copy(flatten(hTh), TP[:, 0]).then_inc(hh_done, 1)
                act.dma_start(hb[:, s], h_t[(i + 2) % NTILE]).then_inc(h_in[s], 16)

            def root_before(i, s):
                act.wait_ge(var_ready, i)
                nc.scalar.activation(std[:, s:s + 1], ve[:, s:s + 1], ACT.Sqrt).then_inc(std_ready, 1)

            def tile(i, s, first=False):
                act.wait_ge(gu_done, i + 1)
                nc.scalar.activation(sl[:], S[:, 0], ACT.Silu).then_inc(silu_done, 1)
                hi_h(i + 1, 1 - s)
                act.wait_ge(at_done, i + 1)
                nc.scalar.copy(flatten(aTh), TP[:, 1]).then_inc(ah_done, 1)
                if not first:
                    root_before(i, 1 - s)

            hi_h(0, 0)
            tile(0, 0, first=True)
            tile(1, 1)
            with act.Fori(1, HALVES) as j:
                for s in range(2):
                    tile(act.snap(j * 2 + s), s)
            root_before(NTILE, 1)
            act.wait_ge(h_in[0], 16 * (HALVES + 2))
            act.wait_ge(h_in[1], 16 * (HALVES + 1))

        @block.tensor
        def _(pe):
            mm = nc.tensor.matmul

            def mm3(out, ah, al, bh, bl, first, last):
                mm(out, ah, bh, start=first, stop=False)
                mm(out, ah, bl, start=False, stop=False)
                return mm(out, al, bh, start=False, stop=last)

            def transpose_h(i, q, s):
                pe.wait_ge(h_in[s], q * 16 + 16)
                for c in range(MC):
                    ins = nc.tensor.transpose(TP[:, 0, c * P:(c + 1) * P], hb[:, s, c * P:(c + 1) * P], idn[:])
                ins.then_inc(t_done, 1)

            def down(i):
                pe.wait_ge(al_done, i + 1)
                for c in range(MC):
                    ins = mm3(O[:], aTh[:, c], aTl[:, c], wh[:, 2, c], wl[:, 2, c], c == 0, c == MC - 1)
                ins.then_inc(dn_done, 1)

            def tile(i, q, s, before=True, o_used=True):
                pe.wait_ge(hl_done, i + 1)
                for c in range(MC):
                    for w in range(2):
                        ins = mm3(S[:, w], hTh[:, c], hTl[:, c], wh[:, w, c], wl[:, w, c], c == 0, c == MC - 1)
                ins.then_inc(gu_done, 1)
                transpose_h(i + 1, q + s, 1 - s)
                if before:
                    if o_used:
                        pe.wait_ge(o_read, i - 1)
                    down(i - 1)
                pe.wait_ge(act_ready, i + 1)
                for c in range(MC):
                    ins = nc.tensor.transpose(TP[:, 1, c * P:(c + 1) * P], ac[:, c * P:(c + 1) * P], idn[:])
                ins.then_inc(at_done, 1)

            pe.wait_ge(const_in, 16)
            transpose_h(0, 0, 0)
            tile(0, 0, 0, before=False)
            tile(1, 0, 1, o_used=False)
            with pe.Fori(1, HALVES) as j:
                for s in range(2):
                    tile(pe.snap(j * 2 + s), j, s)
            pe.wait_ge(o_read, NTILE - 1)
            down(NTILE - 1)


def build(nc, x, w_aq, w_ak, w_av, w_ao, norm_w, router_w, w1, w2, sg, su, sd, const, out):
    x2_d = nc.dram_tensor("x2_d", (B, T, M), F32).ap()
    h_d = nc.dram_tensor("h_d", (B, T, M), F32).ap()
    y_d = nc.dram_tensor("y_d", ((XT + 1) * P, M), F32).ap()
    with ExitStack() as logits:
        coef = logits.enter_context(nc.sbuf_tensor("coef", [P, NTILE, K + 2], F32))
        topi = logits.enter_context(nc.sbuf_tensor("topi", [P, NTILE, K], U32))
        attention(nc, x, w_aq, w_ak, w_av, w_ao, norm_w, router_w, const, x2_d, h_d, topi, coef)
        with ExitStack() as ctx:
            def keep(name, shape, dt):
                return ctx.enter_context(nc.sbuf_tensor(name, shape, dt))

            slots = keep("slots", [P, NTILE, K], I32)
            ids = keep("ids", [P, XW], I32)
            etab = keep("etab", [P, XW + 1], I32)
            ctab = keep("ctab", [P, E + 1], I32)
            raww = keep("raww", [P, 2, WC], F32)
            wsh, wsl = keep("wsh", [P, 3, MC, M], F32R), keep("wsl", [P, 3, MC, M], F32R)
            dispatch(nc, sg, su, sd, w1, w2, const, topi, slots, coef, ids, etab, ctab, wsh, wsl, raww)
            experts(nc, w1, w2, const, h_d, y_d, ids, etab, ctab, raww)
            finish(nc, const, h_d, x2_d, y_d, out, slots, coef, wsh, wsl)


_INS = ['L0_attn_x', 'L0_attn_w_aq', 'L0_attn_w_ak', 'L0_attn_w_av', 'L0_attn_w_ao', 'L0_ffn_norm_w', 'L0_ffn_router_w',
        'L0_ffn_w1', 'L0_ffn_w2', 'L0_ffn_sg', 'L0_ffn_su', 'L0_ffn_sd']


def _constants():
    import numpy as np

    c = np.zeros((P, C_W), np.float32)
    c[:, C_ID:C_ID + P] = np.eye(P)
    i = np.arange(P)
    c[:, C_MASK:C_MASK + P] = np.where(i[:, None] < i[None, :], MASKED, 0.0)
    c[:, C_TRI:C_TRI + P] = i[:, None] < i[None, :]
    freq = np.power(np.float32(10000.0), -np.arange(HALF, dtype=np.float32) / np.float32(HALF)).astype(np.float32)
    angle = (np.arange(T, dtype=np.float32)[:, None] * freq[None, :]).astype(np.float32).reshape(NT, P, HALF)
    angle = angle.transpose(1, 0, 2).reshape(P, NT * HALF)
    mult = np.float32(D ** -0.25)
    c[:, C_COS:C_COS + NT * HALF] = np.cos(angle) * mult
    c[:, C_SIN:C_SIN + NT * HALF] = np.sin(angle) * mult
    c[:, C_IOTA:C_IOTA + C_TOK - C_IOTA] = np.arange(C_TOK - C_IOTA)
    c[:, C_TOK:C_TOK + NTILE] = np.arange(NTILE)[None, :] * P + i[:, None]
    return c


def kernel(**inputs):
    import numpy as _np
    import concourse.bacc as _bacc
    from concourse import mybir as _mybir
    from concourse.bass_utils import run_bass_kernel_spmd as _run

    nc = _bacc.Bacc("TRN2", target_bir_lowering=False, num_devices=1)
    arrays, args = {}, []
    named = [(name, _np.ascontiguousarray(inputs[name])) for name in _INS] + [("constants", _constants())]
    for name, a in named:
        arrays[f"in_{name}_dram"] = a
        args.append(nc.dram_tensor(f"in_{name}_dram", a.shape, _mybir.dt.from_np(a.dtype), kind="ExternalInput").ap())
    args.append(nc.dram_tensor("out_0_dram", (B, T, M), _mybir.dt.float32, kind="ExternalOutput").ap())
    build(nc, *args)
    r = _run(nc, [arrays], core_ids=[0])
    return r.results[0]["out_0_dram"]
```
